# Optimizing a Trainium2 kernel written in Bass

```python
import numpy as np
import jax
import jax.numpy as jnp

def _softmax(x, axis=-1):
    return jax.nn.softmax(x, axis=axis)
def _gelu(x):
    return jax.nn.gelu(x, approximate=True)
def _silu(x):
    return jax.nn.silu(x)
def _sigmoid(x):
    return jax.nn.sigmoid(x)
def _layernorm(x, axis=-1, eps=1e-5):
    m = jnp.mean(x, axis=axis, keepdims=True)
    v = jnp.var(x, axis=axis, keepdims=True)
    return (x - m) / jnp.sqrt(v + eps)
def _scatter_add(tgt, idx, src, axis=0):
    return tgt.at[idx].add(src)
def _segment_sum(src, seg, n):
    return jax.ops.segment_sum(src, seg, n)

kernel_name = 'mk_conv_preact_d1_conv_nchw256_7822c6'

def setup_inputs(seed: int = 0):
    np.random.seed(seed)
    _w = jnp.asarray
    def _rec_inputs():
        import jax
        import jax.numpy as jnp
        _gk = jax.random.key(seed)
        x = -8.268e-05 + 0.9999 * jax.random.normal(jax.random.fold_in(_gk, 1), (64, 256, 56, 56), jnp.float32)
        return x
    x = _rec_inputs()
    def _L0_conv_setup():
        import jax, jax.numpy as jnp
        import numpy as np
        from jax import lax
        T = 8
        EPS = 1e-05

        def _branch(x5, w, g, b, axis):
            y = jnp.moveaxis(x5, axis, 1)
            p = jnp.stack([y.max(axis=1), y.mean(axis=1)], axis=1)
            z = lax.conv_general_dilated(p, w, window_strides=(1, 1, 1), padding=[(1, 1), (1, 1), (1, 1)], dimension_numbers=('NCDHW', 'OIDHW', 'NCDHW'))
            mu = z.mean()
            var = ((z - mu) ** 2).mean()
            z = (z - mu) * lax.rsqrt(var + EPS) * g + b
            gate = jax.nn.sigmoid(z)
            return x5 * jnp.moveaxis(gate, 1, axis)
        key = jax.random.key(seed)
        ks = jax.random.split(key, 5)
        x = jax.random.normal(ks[0], (64, 256, 56, 56), jnp.float32)

        def w(k):
            return jax.random.normal(k, (1, 2, 3, 3, 3), jnp.float32) * 0.19
        return {'x': x, 'w_str': w(ks[1]), 'w_sr': w(ks[2]), 'w_trh': w(ks[3]), 'w_trw': w(ks[4]), 'gamma': jnp.ones((4,), jnp.float32), 'beta': jnp.zeros((4,), jnp.float32)}
    _L0_conv_all = _L0_conv_setup()
    _L0_conv_in = {k: v for k, v in _L0_conv_all.items() if k in ('w_str', 'w_sr', 'w_trh', 'w_trw', 'gamma', 'beta', )}
    del _L0_conv_all

    return {
        "x": x,
        "L0_conv_w_str": _L0_conv_in["w_str"],
        "L0_conv_w_sr": _L0_conv_in["w_sr"],
        "L0_conv_w_trh": _L0_conv_in["w_trh"],
        "L0_conv_w_trw": _L0_conv_in["w_trw"],
        "L0_conv_gamma": _L0_conv_in["gamma"],
        "L0_conv_beta": _L0_conv_in["beta"],
    }

def reference(x, L0_conv_w_str, L0_conv_w_sr, L0_conv_w_trh, L0_conv_w_trw, L0_conv_gamma, L0_conv_beta):
    import jax
    import jax.numpy as jnp
    def _L0_conv_ref(x, w_str, w_sr, w_trh, w_trw, gamma, beta):
        import jax, jax.numpy as jnp
        import numpy as np
        from jax import lax
        T = 8
        EPS = 1e-05

        def _branch(x5, w, g, b, axis):
            y = jnp.moveaxis(x5, axis, 1)
            p = jnp.stack([y.max(axis=1), y.mean(axis=1)], axis=1)
            z = lax.conv_general_dilated(p, w, window_strides=(1, 1, 1), padding=[(1, 1), (1, 1), (1, 1)], dimension_numbers=('NCDHW', 'OIDHW', 'NCDHW'))
            mu = z.mean()
            var = ((z - mu) ** 2).mean()
            z = (z - mu) * lax.rsqrt(var + EPS) * g + b
            gate = jax.nn.sigmoid(z)
            return x5 * jnp.moveaxis(gate, 1, axis)
        bn, c, h, w_ = x.shape
        B = bn // T
        x5 = x.reshape(B, T, c, h, w_)
        y1 = _branch(x5, w_str, gamma[0], beta[0], 2)
        y2 = _branch(x5, w_sr, gamma[1], beta[1], 1)
        y3 = _branch(x5, w_trh, gamma[2], beta[2], 3)
        y4 = _branch(x5, w_trw, gamma[3], beta[3], 4)
        out = 0.25 * (y1 + y2 + y3 + y4)
        return out.reshape(bn, c, h, w_)

    def _gn(v, G=32, eps=1e-5):
        B_, C_, H_, W_ = v.shape
        g = v.reshape(B_, G, C_ // G, H_, W_)
        m = jnp.mean(g, axis=(2, 3, 4), keepdims=True)
        s = jnp.var(g, axis=(2, 3, 4), keepdims=True)
        return ((g - m) / jnp.sqrt(s + eps)).reshape(v.shape)

    def _ln_c(v, eps=1e-6):
        m = jnp.mean(v, axis=1, keepdims=True)
        s = jnp.var(v, axis=1, keepdims=True)
        return (v - m) / jnp.sqrt(s + eps)

    def _ln_t(v, eps=1e-5):
        m = jnp.mean(v, axis=-1, keepdims=True)
        s = jnp.var(v, axis=-1, keepdims=True)
        return (v - m) / jnp.sqrt(s + eps)

    def _to_tokens(v):
        B_, C_, H_, W_ = v.shape
        return v.reshape(B_, C_, H_ * W_).transpose(0, 2, 1)
    def _from_tokens(t, like):
        B_, C_, H_, W_ = like.shape
        return t.transpose(0, 2, 1).reshape(B_, C_, H_, W_)

    x = x + _L0_conv_ref(_gn(x), L0_conv_w_str, L0_conv_w_sr, L0_conv_w_trh, L0_conv_w_trw, L0_conv_gamma, L0_conv_beta)
    return x


_drawn_inputs = setup_inputs


def setup_inputs(seed=0):
    import zlib

    import numpy as np

    out = dict(_drawn_inputs(seed))
    spreads = {'L0_conv_gamma': (1.0, 0.6), 'L0_conv_beta': (0.0, 2.0)}
    factors = {'L0_conv_w_str': 45.564}
    for name, (base, spread) in spreads.items():
        noise = np.random.default_rng([zlib.crc32(name.encode()), seed]).standard_normal(out[name].shape)
        drawn = base * np.exp(spread * noise) if base else spread * noise
        out[name] = jnp.asarray(drawn.astype(out[name].dtype))
    for name, factor in factors.items():
        out[name] = (out[name] * factor).astype(out[name].dtype)
    return out
```

```python
from contextlib import ExitStack

import numpy as np

import concourse.bass as bass
from concourse import mybir

F32 = mybir.dt.float32
BF16 = mybir.dt.bfloat16
ALU = mybir.AluOpType
ACT = mybir.ActivationFunctionType
AX = mybir.AxisListType

P = 128
T = 8
HALVES = 2
STEPS = HALVES * T
GROUP = 8
H = W = 56
HW = H * W
EPS_ = 1e-5
SLOTS = 4

CT = 29
NCT = -(-P * HALVES // CT)
CIN = CT + 2
KIN = CIN * 4
MOUT = CT * 4
MLAST = 4 * (P * HALVES - CT * (NCT - 1))
CPAD = CT * NCT + 2
PL2 = (H // 2 + 1) * W
PL34 = (T // 2 + 1) * W
ROW2 = 4 * PL2
ROW34 = 4 * 2 * PL34
ODD = PL2 + W
N2 = H // 4 // 2 * W
IN2 = (H // 4 + 1) * W
N34 = T // 4 * W
UNITS2 = 2 * NCT
RING2, RING34, RING1 = 2, 3, 2
RING = {"2": RING2, "34": RING34, "1": RING1}
RB, CQ = 28, 4
NHB, NO = H // RB, W // CQ
BLK = RB * CQ
NBLK = NHB * NO
PER = 8
NGRP = -(-NBLK // PER)
HCOL = 64
CCOL = 256
CH = 8 * W
CHUNKS = HW // CH
G2 = -(-CHUNKS // 3)
TEAR = H * 2


def dims(base, offset, *pairs):
    return bass.AP(tensor=base.tensor, offset=base.offset + offset, ap=[list(base.ap[0])] + [list(p) for p in pairs])


def units_of_entry():
    u2, u34 = [("2", u) for u in range(UNITS2)], [("34", u) for u in range(NCT)]
    units = []
    while u2 or u34:
        units += u2[:2] + u34[:1]
        u2, u34 = u2[2:], u34[1:]
    units = units[:3] + [("t", 0)] + units[3:] + [("1", 0), ("1", 1)]
    first, last = 4, STEPS - 2
    n = last - first + 1
    return units, [first + q * n // len(units) for q in range(len(units))]


def build(nc, x, w_str, w_sr, w_trh, w_trw, gamma, beta, k_sq, k_wh, k_mask, k_mask1, k_kind, k_gate, k_sel, out):
    B = x.shape[0] // T
    xt = x.rearrange("(b t) (g c) h w -> b g t c (h w)", t=T, c=P)
    ot = out.rearrange("(b t) (g c) h w -> b g t c (h w)", t=T, c=P)
    ZC = B * T * HW // P
    units, unit_step = units_of_entry()
    NU = len(units)
    counted = [q for q in range(NU) if units[q][0] != "t"]

    ctx = ExitStack()
    with ctx:
        def sem(name):
            return ctx.enter_context(nc.semaphore(name))

        p2_d = nc.dram_tensor("p2_d", [B, CPAD, ROW2], F32)
        p34_d = nc.dram_tensor("p34_d", [B, CPAD, ROW34], F32)
        p1_d = nc.dram_tensor("p1_d", [B, 2, NHB, T + 2, HW // NHB], F32)
        z2_d = nc.dram_tensor("z2_d", [B, CT * NCT, HW], F32)
        z34_d = nc.dram_tensor("z34_d", [B, CT * NCT, T * 2 * W], F32)
        z1_d = nc.dram_tensor("z1_d", [B, T, H, W], F32)
        g1_d = nc.dram_tensor("g1_d", [3, B * T * HW], BF16)
        st_d = nc.dram_tensor("st_d", [B, HALVES, P, 2 * T], F32)

        words = 212800 // 4
        S = ctx.enter_context(nc.sbuf_tensor("S", [P, words], F32))

        def taker(at, end):
            place = [at]

            def take(*shape, dt=F32):
                n = int(np.prod(shape))
                n = n if dt == F32 else n // 2
                at = (place[0] + 7) // 8 * 8
                place[0] = at + n
                assert at + n <= end, (at + n, end)
                v = S[:, at:at + n]
                if dt != F32:
                    v = v.bitcast(dt)
                if len(shape) > 1:
                    names = "abcdef"[:len(shape)]
                    v = v.rearrange(f"p ({' '.join(names)}) -> p {' '.join(names)}", **dict(zip(names, shape)))
                return v
            return take, place

        take, used = taker(0, words)
        V = take(SLOTS, HW)
        IDN = take(P)
        GRP = take(3, P)
        ONES = take(P)
        EPS = take(1)
        CONST = take(2)
        GB = take(8)
        KG = take(24)
        S2 = take(B, UNITS2, 6)
        S34 = take(2, B, NCT, 6)
        S1 = take(B, HALVES, 6)
        FIN = take(4, 4)
        FT = take(4, 4)
        FM = take(4, 2)
        FD = take(4, 2)
        FV = take(4)
        SCL = take(2, 4)
        common_end = used[0]
        ACC = take(HALVES, 2, 2 * PL2)
        VT = take(2, NBLK, P)
        JUNK = take(HW, dt=BF16)
        P34 = take(HALVES, 8, PL34)
        IN2B = take(RING2, IN2)
        IN34B = take(RING34, 2 * PL34)
        IN1B = take(2, (T // 2 + 2) * W)
        CM = take(2, HALVES, T * NBLK)
        CB = take(2, T * NBLK)
        Z2B = take(RING2, N2)
        Z34B = take(RING34, 2 * N34)
        Z1B = take(2, T // 2 * W)
        P1T = Z1B.rearrange("p a n -> p (a n)")
        BAND = take(3, 9, MOUT)
        BAND1 = take(9, H)
        WH = take(RB * 2)
        RM = take(HALVES, 2, T)
        SUM = take(2)
        CEN = take(2)
        SQ = take(2)
        ER = take(2)
        SG = take(2)
        NMR = take(2)
        MD = take(2, 2)
        phase1_end = used[0]
        take3, _ = taker(IN2B.offset, IN2B.offset + RING2 * IN2)
        MASK = take3(3, CT)
        MASK1 = take3(3, H)
        KIND = take3(8)
        WB = take3(4, 54)
        WK = take3(27)
        R9 = take3(3, 9, 3)
        RP = take3(3, 8, 3)
        TMP = take3(9 * H)
        take2, _ = taker(common_end, phase1_end)
        AB = take2(2, HW)
        G2Z = take2(HW)
        G2F = take2(HW)
        G2P = take2(2, 3, HW, dt=BF16)
        SELR = take2(2, HW, dt=BF16)
        G34Z = take2(T * 2 * W)
        G34F = take2(T * 2 * W)
        G34P = take2(2, 3, T * 2 * W, dt=BF16)
        GT = take2(2, 3, P, dt=BF16)
        IDB = take2(P, dt=BF16)
        RM2 = take2(2, 2, T)
        R4 = take2(2, T)
        take4, _ = taker(AB.offset, AB.offset + 2 * HW)
        Z1F = take4(ZC)
        Z1P = take4(3, ZC, dt=BF16)

        PS = ctx.enter_context(nc.psum_tensor("PS", [P, 8, 512], F32))
        SUMS, STAT, CONV = 4, 5, 6

        consts_in = sem("consts_in")
        x_in = [sem(f"x_in{i}") for i in range(SLOTS)]
        zeros_up = sem("zeros_up")
        pads_out = sem("pads_out")
        pool_init = sem("pool_init")
        dve_init = sem("dve_init")
        chain = sem("chain")
        bands_up = sem("bands_up")
        summed = sem("summed")
        centred = sem("centred")
        squared = sem("squared")
        mean_mm = sem("mean_mm")
        md_copied = sem("md_copied")
        e_up = sem("e_up")
        var_mm = sem("var_mm")
        sigma = sem("sigma")
        r_up = sem("r_up")
        rm_up = sem("rm_up")
        v_up = sem("v_up")
        transposed = sem("transposed")
        vt_up = sem("vt_up")
        c_summed = sem("c_summed")
        hw_summed = sem("hw_summed")
        sums_out = sem("sums_out")
        maxed = sem("maxed")
        t_summed = sem("t_summed")
        c_maxed = sem("c_maxed")
        cs_up = sem("cs_up")
        cb_up = sem("cb_up")
        p2_out = [sem(f"p2_out{g}") for g in range(HALVES)]
        p34_out = [sem(f"p34_out{g}") for g in range(HALVES)]
        st_out = [sem(f"st_out{g}") for g in range(HALVES)]
        in2 = [sem(f"in2_{i}") for i in range(RING2)]
        in34 = [sem(f"in34_{i}") for i in range(RING34)]
        in1 = [sem(f"in1_{i}") for i in range(2)]
        unit_mm = sem("unit_mm")
        unit_out = sem("unit_out")
        unit_stat = sem("unit_stat")
        z2_out = [sem(f"z2_out{i}") for i in range(RING2)]
        z34_out = [sem(f"z34_out{i}") for i in range(RING34)]
        z1_out = [sem(f"z1_out{i}") for i in range(2)]
        p1_out = sem("p1_out")
        fin_up = sem("fin_up")
        fin_mm = sem("fin_mm")
        fin_sg = sem("fin_sg")
        scl_up = sem("scl_up")
        sel_in = sem("sel_in")
        sel_up = sem("sel_up")
        z1_in = sem("z1_in")
        g1_up = sem("g1_up")
        g1_split = sem("g1_split")
        g1_out = sem("g1_out")
        z2_in = sem("z2_in")
        z34_in = sem("z34_in")
        rm_in = sem("rm_in")
        g2_up = sem("g2_up")
        g34_up = sem("g34_up")
        pool = sem("pool")
        row_in = [sem(f"row_in{i}") for i in range(2)]
        y_in = [sem(f"y_in{i}") for i in range(SLOTS)]
        gt_mm = sem("gt_mm")
        gt_up = sem("gt_up")
        gates_mm = sem("gates_mm")
        a_up = sem("a_up")
        scaled = sem("scaled")
        done = sem("done")
        y_out = [sem(f"y_out{i}") for i in range(SLOTS)]

        CONSTS = 16 * 13
        PADS = 16 * (2 * (1 + B) + 2)

        def at(b, i):
            return b * STEPS + i

        def later(e):
            return not isinstance(e, int) or e > 0

        def lagged(i, lag, first, last):
            return not (first and i < lag) and not (last and i >= lag)

        def run(eng, step):
            for i in range(STEPS):
                step(0, i, True, False)
            with eng.Fori(1, B) as b:
                for i in range(STEPS):
                    step(b, i, False, False)
            for i in range(STEPS):
                step(B, i, False, True)

        def here(i):
            return [(q, *units[q]) for q in range(NU) if unit_step[q] == i]

        def early(i):
            return here(i)[:-1]

        def late(i):
            return here(i - 1)[-1:] if i else []

        def q_of(kind, u):
            return units.index((kind, u))

        def frame_slot(t):
            return t % 2, (t + 1) // 2

        def pooled(g, kind, t, branch):
            p, q = frame_slot(t)
            return P34[:, g, (kind * 2 + p) * 2 + branch, q * W:(q + 1) * W]

        def plane(g, kind):
            return dims(ACC, (g * 2 + kind) * 2 * PL2, (ODD, 2), (W, H // 2), (1, W))

        def tile_rows(slot):
            return V[:, slot, :].rearrange("p (q e w) -> p e q w", e=2, w=W)

        def blocks(slot, k):
            return dims(V[:, slot, :], k // NO * RB * W + k % NO, (NO, BLK))

        def over_c(kind, g, t):
            return dims(CM, ((kind * HALVES + g) * T + t // 4 * 4) * NBLK + t % 4 * NO, (4 * NO, NHB), (1, NO))

        block = ctx.enter_context(nc.Block())

        @block.sync
        def _(sp):
            small = [(IDN, k_sq[:, 0, :]), (GRP, k_sq[:, 1:4, :]), (WH[0:BLK], k_wh), (MASK[0:KIN], k_mask),
                     (MASK1[0:2 * H], k_mask1), (KIND, k_kind),
                     (KG, k_gate),
                     (GB[:, 0:4], gamma.rearrange("(o n) -> o n", o=1).broadcast_to([P, 4])),
                     (GB[:, 4:8], beta.rearrange("(o n) -> o n", o=1).broadcast_to([P, 4]))]
            small += [(WB[:, i, :], w.rearrange("o k a b c -> o (k a b c)").broadcast_to([P, 54]))
                      for i, w in enumerate((w_str, w_sr, w_trh, w_trw))]

            def pads():
                zero = VT.rearrange("p a n c -> p (a n c)")
                sp.wait_ge(zeros_up, 1)
                for d, n in ((p2_d, ROW2), (p34_d, ROW34)):
                    sp.dma_start(d[:, 0, :], zero[0:B, 0:n]).then_inc(pads_out, 16)
                    for b in range(B):
                        sp.dma_start(d[b, P * HALVES + 1:CPAD, :],
                                     zero[0:CPAD - P * HALVES - 1, 0:n]).then_inc(pads_out, 16)
                for tt in (0, T + 1):
                    sp.dma_start(p1_d[:, :, :, tt, :].rearrange("b k h n -> (b k h) n"),
                                 zero[0:2 * NHB * B, 0:HW // NHB]).then_inc(pads_out, 16)

            def unit_in(e, kind, u):
                if kind == "t":
                    return
                ring = RING[kind]
                if u >= ring:
                    sp.wait_ge(unit_mm, e * NU + q_of(kind, u - ring) + 1)
                if kind == "2":
                    ct, kc = u // 2, u % 2
                    rows = p2_d[e, CT * ct:CT * ct + CIN, :].rearrange("c (k n) -> (c k) n", k=4)
                    sp.dma_start(IN2B[0:KIN, u % RING2, :], rows[:, kc * 2 * N2:kc * 2 * N2 + IN2]).then_inc(in2[u % RING2], 16)
                elif kind == "34":
                    rows = p34_d[e, CT * u:CT * u + CIN, :].rearrange("c (k n) -> (c k) n", k=4)
                    sp.dma_start(IN34B[0:KIN, u % RING34, :], rows).then_inc(in34[u % RING34], 16)
                else:
                    sp.wait_ge(p1_out, (e + 1) * 128)
                    for k in range(2):
                        for hb in (1, 0):
                            rows = p1_d[e, k, hb, T // 2 * u:T // 2 * u + T // 2 + 2, :].rearrange(
                                "t (o h q) -> h (t o) q", o=NO, q=CQ)
                            sp.dma_start(IN1B[H * k + RB * hb:H * k + RB * (hb + 1), u, :].rearrange(
                                "h (n q) -> h n q", q=CQ), rows).then_inc(in1[u], 16)

            def unit_store(e, q, kind, u):
                sp.wait_ge(unit_out, e * NU + q + 1)
                if kind == "2":
                    ct, kc = u // 2, u % 2
                    rows = z2_d[e, CT * ct:CT * (ct + 1), :].rearrange("c (j n) -> (c j) n", j=4)
                    sp.dma_start(rows[:, kc * N2:(kc + 1) * N2], Z2B[0:MOUT, u % RING2, :]).then_inc(z2_out[u % RING2], 16)
                elif kind == "34":
                    rows = z34_d[e, CT * u:CT * (u + 1), :].rearrange("c (j n) -> (c j) n", j=4)
                    sp.dma_start(rows, Z34B[0:MOUT, u % RING34, :]).then_inc(z34_out[u % RING34], 16)
                elif kind == "1":
                    sp.dma_start(z1_d[e, T // 2 * u:T // 2 * (u + 1)].rearrange("t h w -> h t w"),
                                 Z1B[0:H, u, :].rearrange("h (t w) -> h t w", w=W)).then_inc(z1_out[u], 16)
                else:
                    m = T // 2 * NO
                    for k in range(2):
                        for th in range(2):
                            for hb in range(NHB):
                                rows = p1_d[e, k, hb, 1 + T // 2 * th:1 + T // 2 * (th + 1), :].rearrange(
                                    "t (o n) -> (t o) n", o=NO)
                                src = P1T[hb * m:(hb + 1) * m, (k * 2 + th) * BLK:(k * 2 + th + 1) * BLK]
                                sp.dma_start(rows, src).then_inc(p1_out, 16)

            def step1(b, i, first, last):
                if not last:
                    slot, g, t, n = i % SLOTS, i // T, i % T, at(b, i)
                    if not (first and i < SLOTS):
                        sp.wait_ge(maxed, n - SLOTS + 1)
                        sp.wait_ge(t_summed, n - SLOTS + 1)
                        sp.wait_ge(c_summed, n - SLOTS + 1)
                    sp.dma_start(V[:, slot, :], xt[b, g, t]).then_inc(x_in[slot], 16)
                if first and i == 0:
                    for dst, src in small:
                        sp.dma_start(dst, src).then_inc(consts_in, 16)
                if first and i == 2:
                    pads()
                g = {T + 2: 0, 2: 1}.get(i)
                if (g == 0 and not last) or (g == 1 and not first):
                    e = b if g == 0 else b - 1
                    n = at(e, T * (g + 1))
                    sp.wait_ge(sums_out, 3 * n)
                    sp.wait_ge(maxed, n)
                    sp.wait_ge(t_summed, n)
                    sp.wait_ge(rm_up, n)
                    sp.dma_start(p2_d[e, 1 + P * g:1 + P * (g + 1), :],
                                 ACC[:, g].rearrange("p k n -> p (k n)")).then_inc(p2_out[g], 16)
                    sp.dma_start(p34_d[e, 1 + P * g:1 + P * (g + 1), :],
                                 P34[:, g].rearrange("p k n -> p (k n)")).then_inc(p34_out[g], 16)
                    sp.dma_start(st_d[e, g], RM[:, g].rearrange("p a n -> p (a n)")).then_inc(st_out[g], 16)
                if first:
                    return
                e = b - 1
                if i == 4:
                    sp.wait_ge(pads_out, PADS)
                    for g in range(HALVES):
                        sp.wait_ge(p2_out[g], (e + 1) * 16)
                        sp.wait_ge(p34_out[g], (e + 1) * 16)
                if i:
                    for q, kind, u in here(i - 1):
                        unit_store(e, q, kind, u)
                for q, kind, u in here(i):
                    unit_in(e, kind, u)

            run(sp, step1)

            for s in z2_out:
                sp.wait_ge(s, 16 * B * UNITS2 // RING2)
            for s in z34_out:
                sp.wait_ge(s, 16 * B * NCT // RING34)
            for s in z1_out:
                sp.wait_ge(s, 16 * B)
            for g in range(HALVES):
                sp.wait_ge(st_out[g], 16 * B)
            sp.wait_ge(unit_stat, B * len(counted))
            sp.wait_ge(unit_mm, B * NU)
            sp.wait_ge(c_maxed, B * STEPS)
            sp.wait_ge(hw_summed, B * STEPS)
            sp.wait_ge(p1_out, B * 128)
            sp.dma_start(G2F[0:TEAR, :], k_sel).then_inc(sel_in, 16)
            sp.dma_start(Z1F, z1_d.rearrange("b t h w -> (b t h w)").rearrange("(p n) -> p n", p=P)).then_inc(z1_in, 16)
            g1_rows = g1_d.rearrange("s (n c) -> n s c", c=HW)

            def step2(b, i, first, last):
                n, g, t = at(b, i), i // T, i % T
                if not last and t == 0:
                    if later(b) or g:
                        sp.wait_ge(pool, 9 * (b * HALVES + g))
                    sp.dma_start(G2Z, z2_d[b, P * g:P * (g + 1), :]).then_inc(z2_in, 16)
                    sp.dma_start(G34Z, z34_d[b, P * g:P * (g + 1), :]).then_inc(z34_in, 16)
                if not last and t == 2:
                    if not first:
                        sp.wait_ge(done, n - 10)
                    sp.dma_start(RM2[:, g].rearrange("p a n -> p (a n)"), st_d[b, g]).then_inc(rm_in, 16)
                if lagged(i, 10, first, last):
                    j = (i - 10) % STEPS
                    e = b if i >= 10 else b - 1
                    sp.wait_ge(done, n - 9)
                    sp.dma_start(ot[e, j // T, j % T], V[:, j % SLOTS, :]).then_inc(y_out[j % SLOTS], 16)
                if first and i == 8:
                    sp.wait_ge(g1_split, 1)
                    for s in range(3):
                        sp.dma_start(g1_d[s].rearrange("(p n) -> p n", p=P), Z1P[:, s, :]).then_inc(g1_out, 16)
                    sp.wait_ge(g1_out, 48)
                    sp.wait_ge(sel_up, 1)
                if lagged(i, 8, first, last):
                    j = (i - 8) % STEPS
                    e = b if i >= 8 else b - 1
                    if not (first and i < 10):
                        sp.wait_ge(gates_mm, (n - 9) * G2)
                    sp.dma_start(SELR[TEAR:TEAR + 3, j % 2, :], g1_rows[e * T + j % T]).then_inc(row_in[j % 2], 16)
                if lagged(i, 7, first, last):
                    j = (i - 7) % STEPS
                    e = b if i >= 7 else b - 1
                    if not (first and i < 11):
                        sp.wait_ge(y_out[j % SLOTS], (e * (STEPS // SLOTS) + j // SLOTS) * 16)
                    sp.dma_start(V[:, j % SLOTS, :], xt[e, j // T, j % T]).then_inc(y_in[j % SLOTS], 16)

            run(sp, step2)
            for s in y_out:
                sp.wait_ge(s, 16 * B * STEPS // SLOTS)

        @block.gpsimd
        def _(eng):
            nc.gpsimd.memset(VT.rearrange("p a n c -> p (a n c)"), 0.0).then_inc(zeros_up, 1)
            nc.gpsimd.memset(CONST[:, 0:1], 0.0).then_inc(pool_init, 1)
            nc.gpsimd.memset(CONST[:, 1:2], 0.25).then_inc(pool_init, 1)
            eng.wait_ge(pool_init, 2)

            def step1(b, i, first, last):
                if not lagged(i, 2, first, last):
                    return
                j, n = (i - 2) % STEPS, at(b, i - 2)
                g, t = j // T, j % T
                eng.wait_ge(v_up, n + 1)
                if t == 0:
                    if not first:
                        eng.wait_ge(p2_out[g], b * 16)
                    nc.gpsimd.tensor_tensor(plane(g, 1), tile_rows(j % SLOTS),
                                            dims(CONST, 0, (0, 2), (0, H // 2), (0, W)), ALU.add).then_inc(t_summed, 1)
                else:
                    eng.wait_ge(t_summed, n)
                    nc.gpsimd.tensor_tensor(plane(g, 1), plane(g, 1), tile_rows(j % SLOTS),
                                            ALU.add).then_inc(t_summed, 1)

            run(eng, step1)

            def step2(b, i, first, last):
                g, t = i // T, i % T
                if last or t != 4:
                    return
                e, n = b * HALVES + g, at(b, i)
                if not first:
                    eng.wait_ge(gates_mm, (n - 12) * G2)
                    eng.wait_ge(a_up, (n - 12) * G2)
                eng.wait_ge(g2_up, e + 1)
                eng.wait_ge(g34_up, e + 1)
                k = 9 * e
                for full, rest, parts in ((G2F, G2Z, G2P[:, g]), (G34F, G34Z, G34P[:, g])):
                    zero = dims(CONST, 0, (0, full.shape[-1]))
                    nc.gpsimd.tensor_tensor(parts[:, 0, :], full, zero, ALU.add).then_inc(pool, 1)
                    eng.wait_ge(pool, k + 1)
                    nc.gpsimd.tensor_tensor(rest, full, parts[:, 0, :], ALU.subtract).then_inc(pool, 1)
                    eng.wait_ge(pool, k + 2)
                    nc.gpsimd.tensor_tensor(parts[:, 1, :], rest, zero, ALU.add).then_inc(pool, 1)
                    eng.wait_ge(pool, k + 3)
                    nc.gpsimd.tensor_tensor(parts[:, 2, :], rest, parts[:, 1, :], ALU.subtract).then_inc(pool, 1)
                    k = k + 4
                eng.wait_ge(rm_in, (e + 1) * 16)
                nc.gpsimd.tensor_tensor(R4[:, g, :], RM2[:, g, 1, :], dims(CONST, 1, (0, T)), ALU.mult).then_inc(pool, 1)

            run(eng, step2)

        @block.scalar
        def _(act):
            def unit(e, q, kind, u):
                act.wait_ge(unit_mm, e * NU + q + 1)
                src = PS[:, CONV + q % 2, :]
                if kind == "t":
                    for s in z1_out:
                        act.wait_ge(s, e * 16)
                    act.wait_ge(unit_stat, e * len(counted))
                    nc.scalar.copy(P1T[0:BLK], src[0:BLK, 0:4 * BLK]).then_inc(unit_out, 1)
                    return
                ring = RING[kind]
                outs = {"2": z2_out, "34": z34_out, "1": z1_out}[kind]
                per = {"2": UNITS2, "34": NCT, "1": 2}[kind] // ring
                act.wait_ge(outs[u % ring], (e * per + u // ring) * 16)
                before = counted.index(q_of(kind, u - ring)) + 1 if u >= ring else 0
                act.wait_ge(unit_stat, e * len(counted) + before)
                dst, m, width = {"2": (Z2B, MOUT, N2), "34": (Z34B, MOUT, 2 * N34), "1": (Z1B, H, T // 2 * W)}[kind]
                dst, src = dst[0:m, u % ring, :], src[0:m, 0:width]
                if kind == "1":
                    dst = dst.rearrange("p (t q o) -> p t o q", q=CQ, o=NO)
                    src = src.rearrange("p (t o q) -> p t o q", q=CQ, o=NO)
                nc.scalar.copy(dst, src).then_inc(unit_out, 1)

            act.wait_ge(dve_init, 1)

            def step1(b, i, first, last):
                n = at(b, i)
                if lagged(i, 2, first, last):
                    j, m = (i - 2) % STEPS, at(b, i - 2)
                    if first and i == 2:
                        act.wait_ge(pads_out, PADS)
                    if not (first and i < 4):
                        act.wait_ge(c_maxed, m - 1)
                        act.wait_ge(hw_summed, m - 1)
                    for gr in range(NGRP):
                        act.wait_ge(transposed, m * NGRP + gr + 1)
                        nb = min(PER, NBLK - PER * gr)
                        src = dims(PS[:, :, :], gr % 2 * 1024, (1, nb * P))[0:BLK]
                        nc.scalar.copy(VT[0:BLK, j % 2, PER * gr:PER * gr + nb, :].rearrange("p n c -> p (n c)"),
                                       src).then_inc(vt_up, 1)
                if not last:
                    slot, par = i % SLOTS, i % 2
                    act.wait_ge(x_in[slot], (b * (STEPS // SLOTS) + i // SLOTS + 1) * 16)
                    if not (first and i == 0):
                        act.wait_ge(squared, n)
                    nc.scalar.activation(JUNK, V[:, slot, :], ACT.Copy,
                                         accum_out=SUM[:, par:par + 1]).then_inc(summed, 1)
                    act.wait_ge(summed, n + 1)
                    nc.scalar.mul(CEN[:, par:par + 1], SUM[:, par:par + 1], -1.0 / (HW * W)).then_inc(centred, 1)
                if not first:
                    for q, kind, u in late(i):
                        unit(b - 1, q, kind, u)
                if lagged(i, 1, first, last):
                    pp = (i - 1) % 2
                    act.wait_ge(var_mm, n)
                    nc.scalar.activation(SG[:, pp:pp + 1], PS[:, STAT, 2:3], ACT.Sqrt, bias=EPS).then_inc(sigma, 1)
                if not last:
                    act.wait_ge(centred, n + 1)
                    nc.scalar.activation(JUNK, V[:, slot, :], ACT.Square, scale=1.0 / W, bias=CEN[:, par:par + 1],
                                         accum_out=SQ[:, par:par + 1]).then_inc(squared, 1)
                if lagged(i, 1, first, last):
                    j = (i - 1) % STEPS
                    act.wait_ge(rm_up, n)
                    v = V[:, j % SLOTS, :]
                    nc.scalar.activation(v, v, ACT.Identity, scale=RM[:, j // T, 1, j % T:j % T + 1],
                                         bias=NMR[:, j % 2:j % 2 + 1]).then_inc(v_up, 1)
                if lagged(i, 2, first, last):
                    j, m = (i - 2) % STEPS, at(b, i - 2)
                    g, t = j // T, j % T
                    p, q = frame_slot(t)
                    act.wait_ge(hw_summed, m + 1)
                    if t == 0 and not first:
                        act.wait_ge(p34_out[g], b * 16)
                    nc.scalar.copy(pooled(g, 1, t, 1), PS[:, SUMS, 0:H]).then_inc(sums_out, 1)
                    nc.scalar.copy(pooled(g, 1, t, 0).rearrange("p (q o) -> p o q", q=CQ),
                                   PS[:, SUMS, HCOL:HCOL + W].rearrange("p (o q) -> p o q", q=CQ)).then_inc(sums_out, 1)
                    if t == 0 and g == 0 and not first:
                        act.wait_ge(cs_up, b)
                    nc.scalar.copy(over_c(1, g, t)[0:BLK], dims(PS[:, :, :], SUMS * 512 + CCOL, (NO, NHB), (1, NO))[0:BLK]
                                   ).then_inc(sums_out, 1)
                if not first:
                    for q, kind, u in early(i):
                        unit(b - 1, q, kind, u)

            run(act, step1)

            act.wait_ge(fin_up, 3)
            nc.scalar.activation(FT[:, 0, :], FV, ACT.Sqrt, bias=EPS).then_inc(fin_sg, 1)
            act.wait_ge(scl_up, 1)

            def gate(out, in_, branch):
                return nc.scalar.activation(out, in_, ACT.Sigmoid, scale=SCL[:, 0, branch:branch + 1],
                                            bias=SCL[:, 1, branch:branch + 1])

            act.wait_ge(z1_in, 16)
            gate(Z1F, Z1F, 0).then_inc(g1_up, 1)
            act.wait_ge(sel_up, 1)

            def step2(b, i, first, last):
                g, t = i // T, i % T
                e = b * HALVES + g
                if not last and t == 1:
                    if later(b) or g:
                        act.wait_ge(pool, 9 * e)
                    act.wait_ge(z2_in, (e + 1) * 16)
                    gate(G2F.rearrange("p (k j w) -> p j k w", j=4, w=W),
                         G2Z.rearrange("p (j k w) -> p j k w", j=4, w=W), 1).then_inc(g2_up, 1)
                if not last and t == 2:
                    act.wait_ge(z34_in, (e + 1) * 16)
                    for s in range(2):
                        ins = gate(dims(G34F, s * W, (4 * W, 4), (2 * W, 2), (1, W)),
                                   dims(G34Z, s * N34, (2 * N34, 4), (W, 2), (1, W)), 2 + s)
                    ins.then_inc(g34_up, 1)
                if lagged(i, 9, first, last):
                    j, m = (i - 9) % STEPS, at(b, i - 9)
                    if not (first and i < 11):
                        act.wait_ge(scaled, m - 1)
                    for gr in range(G2):
                        act.wait_ge(gates_mm, m * G2 + gr + 1)
                        nb = min(3, CHUNKS - 3 * gr)
                        bank = (3 * j + gr) % 2 * 3
                        nc.scalar.activation(
                            AB[:, j % 2, 3 * CH * gr:3 * CH * gr + nb * CH].rearrange("p (n c) -> p n c", c=CH),
                            PS[:, bank:bank + nb, 0:CH], ACT.Identity, scale=R4[:, j // T, j % T:j % T + 1],
                            bias=ONES[:, 0:1]).then_inc(a_up, 1)

            run(act, step2)

        @block.vector
        def _(dve):
            count = [0]

            def link(ins):
                count[0] += 1
                ins.then_inc(chain, 1)
                dve.wait_ge(chain, count[0])

            link(nc.vector.memset(dims(ACC, PL2 - W, (2 * PL2, 2 * HALVES), (1, 2 * W)), 0.0))
            link(nc.vector.memset(P34.rearrange("p a b c -> p (a b c)"), 0.0))
            link(nc.vector.memset(ONES, 1.0))
            link(nc.vector.memset(FIN.rearrange("p a b -> p (a b)"), 0.0))
            nc.vector.memset(EPS, EPS_).then_inc(dve_init, 1)

            dve.wait_ge(consts_in, CONSTS)

            def weights(i, kind0, kind1):
                link(nc.vector.tensor_scalar(WK, WB[:, i, 0:27], KIND[:, kind0:kind0 + 1], None, ALU.mult))
                link(nc.vector.scalar_tensor_tensor(out=WK, in0=WB[:, i, 27:54], scalar=KIND[:, kind1:kind1 + 1],
                                                    in1=WK, op0=ALU.mult, op1=ALU.add))

            for branch in range(3):
                weights(1 + branch, 0, 1 if branch == 0 else 2)
                link(nc.vector.memset(R9.rearrange("p a b c -> p (a b c)"), 0.0))
                for a in range(3):
                    src = dims(WK, 3 * a, (9, 3), (1, 3)) if branch == 0 else dims(WK, 9 * a, (3, 3), (1, 3))
                    link(nc.vector.tensor_copy(R9[:, :, 5 - a, :], src))
                link(nc.vector.tensor_scalar(RP.rearrange("p a b c -> p a (b c)"), dims(R9, 0, (27, 3), (1, 24)),
                                             KIND[:, 3:4], None, ALU.mult))
                link(nc.vector.scalar_tensor_tensor(
                    out=RP.rearrange("p a b c -> p a (b c)"), in0=dims(R9, 3, (27, 3), (1, 24)), scalar=KIND[:, 4:5],
                    in1=RP.rearrange("p a b c -> p a (b c)"), op0=ALU.mult, op1=ALU.add))
                for qo in range(3):
                    band = dims(BAND, (branch * 9 + qo * 3) * MOUT, (MOUT, 3), (4, CT), (1, 4))[0:KIN]
                    tmp = dims(TMP, 0, (MOUT, 3), (4, CT), (1, 4))[0:KIN]
                    for dc in range(3):
                        link(nc.vector.tensor_tensor(tmp if dc else band,
                                                     dims(MASK, dc * CT, (0, 3), (1, CT), (0, 4))[0:KIN],
                                                     dims(RP, dc * 24 + (4 - 2 * qo) * 3, (1, 3), (0, CT), (3, 4))[0:KIN],
                                                     ALU.mult))
                        if dc:
                            link(nc.vector.tensor_tensor(band, band, tmp, ALU.add))
            weights(0, 5, 6)
            band = BAND1[0:2 * H].rearrange("p a b -> p (a b)")
            for dh in range(3):
                link(nc.vector.tensor_tensor(
                    (TMP[0:2 * H] if dh else band).rearrange("p (a b c) -> p a b c", a=3, b=3),
                    dims(MASK1, dh * H, (0, 3), (0, 3), (1, H))[0:2 * H],
                    dims(WK, dh * 3, (9, 3), (1, 3), (0, H))[0:2 * H], ALU.mult))
                if dh:
                    link(nc.vector.tensor_tensor(band, band, TMP[0:2 * H], ALU.add))
            nc.vector.memset(TMP[:, 0:1], 0.0).then_inc(bands_up, 1)

            def stat(e, q, kind, u):
                if kind == "t":
                    return
                dve.wait_ge(unit_out, e * NU + q + 1)
                if kind == "2":
                    ins = nc.vector.bn_stats(S2[0:MOUT, e, u, :], Z2B[0:MOUT, u % RING2, :])
                elif kind == "34":
                    for s in range(2):
                        ins = nc.vector.bn_stats(S34[0:MOUT, s, e, u, :], Z34B[0:MOUT, u % RING34, s * N34:(s + 1) * N34])
                else:
                    ins = nc.vector.bn_stats(S1[0:H, e, u, :], Z1B[0:H, u, :])
                ins.then_inc(unit_stat, 1)

            def step1(b, i, first, last):
                n = at(b, i)
                if i == 2 and not first:
                    dve.wait_ge(sums_out, 3 * at(b, 0))
                    nc.vector.tensor_tensor(CB[0:BLK, 1, :], CM[0:BLK, 1, 0, :], CM[0:BLK, 1, 1, :],
                                            ALU.add).then_inc(cs_up, 1)
                late_tile = lagged(i, 2, first, last)
                if late_tile:
                    j, m = (i - 2) % STEPS, at(b, i - 2)
                    g, t, slot = j // T, j % T, j % SLOTS
                    dve.wait_ge(v_up, m + 1)
                    if t == 0 and not first:
                        dve.wait_ge(p34_out[g], b * 16)
                        dve.wait_ge(p2_out[g], b * 16)
                    tile = V[:, slot, :]
                    nc.vector.tensor_reduce(pooled(g, 0, t, 1), tile.rearrange("p (h w) -> p h w", w=W), AX.X, ALU.max)
                    nc.vector.tensor_reduce(pooled(g, 0, t, 0), tile.rearrange("p (h w) -> p w h", w=W), AX.X, ALU.max)
                if lagged(i, 1, first, last):
                    k = (i - 1) % STEPS
                    gk, tk, pk = k // T, k % T, k % 2
                    dve.wait_ge(sigma, n)
                    nc.vector.reciprocal(RM[:, gk, 1, tk:tk + 1], SG[:, pk:pk + 1]).then_inc(r_up, 1)
                    dve.wait_ge(r_up, n)
                    nc.vector.tensor_tensor(NMR[:, pk:pk + 1], RM[:, gk, 0, tk:tk + 1], RM[:, gk, 1, tk:tk + 1],
                                            ALU.mult).then_inc(rm_up, 1)
                if late_tile:
                    if t == 0:
                        nc.vector.tensor_copy(plane(g, 0), tile_rows(slot)).then_inc(maxed, 1)
                    else:
                        dve.wait_ge(maxed, m)
                        nc.vector.tensor_tensor(plane(g, 0), plane(g, 0), tile_rows(slot), ALU.max).then_inc(maxed, 1)
                if not last:
                    g0, t0, p0 = i // T, i % T, i % 2
                    dve.wait_ge(mean_mm, n + 1)
                    if t0 == 0 and not first:
                        dve.wait_ge(st_out[g0], b * 16)
                    nc.vector.tensor_copy(RM[:, g0, 0, t0:t0 + 1], PS[:, STAT, 0:1]).then_inc(md_copied, 1)
                    nc.vector.tensor_copy(MD[:, p0, 0:1], PS[:, STAT, 1:2]).then_inc(md_copied, 1)
                    dve.wait_ge(md_copied, 2 * n + 2)
                    dve.wait_ge(squared, n + 1)
                    nc.vector.scalar_tensor_tensor(out=ER[:, p0:p0 + 1], in0=MD[:, p0, 0:1], scalar=MD[:, p0, 0:1],
                                                   in1=SQ[:, p0:p0 + 1], op0=ALU.mult, op1=ALU.add).then_inc(e_up, 1)
                if not first:
                    for q, kind, u in late(i):
                        stat(b - 1, q, kind, u)
                if lagged(i, 3, first, last):
                    j, m = (i - 3) % STEPS, at(b, i - 3)
                    dve.wait_ge(vt_up, (m + 1) * NGRP)
                    nc.vector.tensor_reduce(over_c(0, j // T, j % T)[0:BLK],
                                            VT[0:BLK, j % 2].rearrange("p (a n) c -> p a n c", a=NHB),
                                            AX.X, ALU.max).then_inc(c_maxed, 1)
                if i == 2 and not first:
                    dve.wait_ge(c_maxed, at(b, 0))
                    nc.vector.tensor_tensor(CB[0:BLK, 0, :], CM[0:BLK, 0, 0, :], CM[0:BLK, 0, 1, :],
                                            ALU.max).then_inc(cb_up, 1)
                if not first:
                    for q, kind, u in early(i):
                        stat(b - 1, q, kind, u)

            run(dve, step1)

            dve.wait_ge(unit_stat, B * len(counted))
            full = 6 * (UNITS2 - 2)
            link(nc.vector.bn_aggr(FIN[0:H, 0, 0:2], S1[0:H].rearrange("p a b c -> p (a b c)")))
            link(nc.vector.bn_aggr(FIN[0:MOUT, 1, 0:2], dims(S2, 0, (6 * UNITS2, B), (1, full))[0:MOUT]))
            link(nc.vector.bn_aggr(FIN[0:MLAST, 1, 2:4], dims(S2, full, (6 * UNITS2, B), (1, 12))[0:MLAST]))
            for s in range(2):
                at_s = s * B * NCT * 6
                link(nc.vector.bn_aggr(FIN[0:MOUT, 2 + s, 0:2], dims(S34, at_s, (6 * NCT, B), (1, 6 * NCT - 6))[0:MOUT]))
                link(nc.vector.bn_aggr(FIN[0:MLAST, 2 + s, 2:4],
                                       dims(S34, at_s + 6 * NCT - 6, (6 * NCT, B), (1, 6))[0:MLAST]))
            nc.vector.memset(TMP[:, 0:1], 0.0).then_inc(fin_up, 1)
            dve.wait_ge(fin_mm, 1)
            weight = KG[:, 0:16].rearrange("p (a b) -> p a b", a=4)
            link(nc.vector.tensor_tensor(FT, PS[:, STAT, 0:16].rearrange("p (a b) -> p a b", a=4), weight, ALU.mult))
            link(nc.vector.tensor_tensor(FM, FT[:, :, 0:2], FT[:, :, 2:4], ALU.add))
            link(nc.vector.tensor_tensor(FD, dims(FIN, 0, (4, 4), (2, 2)), dims(FM, 0, (2, 4), (0, 2)), ALU.subtract))
            link(nc.vector.tensor_tensor(FD, FD, FD, ALU.mult))
            nc.vector.tensor_tensor(FD, FD, KG[:, 16:24].rearrange("p (a b) -> p a b", a=4), ALU.mult).then_inc(fin_up, 1)
            dve.wait_ge(fin_mm, 2)
            link(nc.vector.tensor_tensor(FT[:, :, 0:2], PS[:, STAT, 16:24].rearrange("p (a b) -> p a b", a=4),
                                         dims(KG, 0, (4, 4), (2, 2)), ALU.mult))
            link(nc.vector.tensor_tensor(FV, FT[:, :, 0], FT[:, :, 1], ALU.add))
            nc.vector.tensor_tensor(FV, FV, FM[:, :, 1], ALU.add).then_inc(fin_up, 1)
            dve.wait_ge(fin_sg, 1)
            link(nc.vector.reciprocal(FT[:, 1, :], FT[:, 0, :]))
            link(nc.vector.tensor_tensor(SCL[:, 0, :], GB[:, 0:4], FT[:, 1, :], ALU.mult))
            link(nc.vector.tensor_tensor(FT[:, 2, :], FM[:, :, 0], SCL[:, 0, :], ALU.mult))
            nc.vector.tensor_tensor(SCL[:, 1, :], GB[:, 4:8], FT[:, 2, :], ALU.subtract).then_inc(scl_up, 1)

            dve.wait_ge(sel_in, 16)
            for a in range(2):
                link(nc.vector.tensor_copy(SELR[0:TEAR, a, :], G2F[0:TEAR, :]))
            link(nc.vector.memset(GT[96:P, :, 0, :], 1.0))
            nc.vector.tensor_copy(IDB, IDN).then_inc(sel_up, 1)
            dve.wait_ge(g1_up, 1)
            link(nc.vector.tensor_copy(Z1P[:, 0, :], Z1F))
            link(nc.vector.tensor_tensor(Z1F, Z1F, Z1P[:, 0, :], ALU.subtract))
            link(nc.vector.tensor_copy(Z1P[:, 1, :], Z1F))
            nc.vector.tensor_tensor(Z1P[:, 2, :], Z1F, Z1P[:, 1, :], ALU.subtract).then_inc(g1_split, 1)

            def step2(b, i, first, last):
                if lagged(i, 8, first, last):
                    j, m = (i - 8) % STEPS, at(b, i - 8)
                    dve.wait_ge(gt_mm, m + 1)
                    if not (first and i < 10):
                        dve.wait_ge(gates_mm, (m - 1) * G2)
                    nc.vector.tensor_copy(GT[0:TEAR, j % 2].rearrange("p a b -> p (a b)"),
                                          PS[0:TEAR, 7, 0:3 * P // 2].bitcast(BF16)).then_inc(gt_up, 1)
                if lagged(i, 9, first, last):
                    j, m = (i - 9) % STEPS, at(b, i - 9)
                    e = b if i >= 9 else b - 1
                    g, t, slot = j // T, j % T, j % SLOTS
                    v, mean = V[:, slot, :], RM2[:, g, 0, t:t + 1]
                    dve.wait_ge(y_in[slot], (e * (STEPS // SLOTS) + j // SLOTS + 1) * 16)
                    dve.wait_ge(rm_in, (e * HALVES + g + 1) * 16)
                    dve.wait_ge(a_up, (m + 1) * G2)
                    nc.vector.scalar_tensor_tensor(out=v, in0=v, scalar=mean, in1=AB[:, j % 2, :], op0=ALU.add,
                                                   op1=ALU.mult).then_inc(scaled, 1)
                    dve.wait_ge(scaled, m + 1)
                    nc.vector.tensor_scalar(v, v, mean, None, ALU.subtract).then_inc(done, 1)

            run(dve, step2)

        @block.tensor
        def _(pe):
            def unit(e, q, kind, u):
                pe.wait_ge(unit_out, e * NU + max(q - 1, 0))
                bank = PS[:, CONV + q % 2, :]
                if kind == "t":
                    pe.wait_ge(cs_up, e + 1)
                    pe.wait_ge(cb_up, e + 1)
                    for kind_ in range(2):
                        for th in range(2):
                            m = kind_ * 2 + th
                            last = nc.tensor.transpose(bank[0:BLK, m * BLK:(m + 1) * BLK],
                                                       CB[0:BLK, kind_, th * BLK:(th + 1) * BLK], IDN[0:BLK, 0:BLK])
                    last.then_inc(unit_mm, 1)
                    return
                order = [(a, dw) for dw in (1, 0, 2) for a in range(3)]
                if kind == "2":
                    pe.wait_ge(in2[u % RING2], (e * (UNITS2 // RING2) + u // RING2 + 1) * 16)
                    jobs = [(bank[0:MOUT, 0:N2], BAND[0:KIN, 0], IN2B[0:KIN, u % RING2, :], 2 * W, W, N2 // W)]
                elif kind == "34":
                    pe.wait_ge(in34[u % RING34], (e * (NCT // RING34) + u // RING34 + 1) * 16)
                    jobs = [(bank[0:MOUT, s * N34:(s + 1) * N34], BAND[0:KIN, 1 + s],
                             IN34B[0:KIN, u % RING34, s * PL34:(s + 1) * PL34], 2 * W, W, N34 // W) for s in range(2)]
                else:
                    pe.wait_ge(in1[u], (e + 1) * 64)
                    number = 0
                    for dw in (1, 0, 2):
                        spans = {0: [(CQ, 0, W - CQ), (1, W - CQ, CQ - 1)], 1: [(0, 0, W)],
                                 2: [(0, CQ, W - CQ), (W - CQ, 1, CQ - 1)]}[dw]
                        for a in range(3):
                            for to, from_, width in spans:
                                dst = bank[0:H, 0:T // 2 * W].rearrange("p (r w) -> p r w", w=W)[:, :, to:to + width]
                                last = nc.tensor.matmul(
                                    dst, BAND1[0:2 * H, a * 3 + dw, :],
                                    dims(IN1B[0:2 * H, u, :], a * W + from_, (W, T // 2), (1, width)),
                                    start=(number == 0), stop=(number == 14), skip_group_check=True)
                                number += 1
                    last.then_inc(unit_mm, 1)
                    return
                for out_, band_, in_, stride, shift, rows in jobs:
                    for number, (a, dw) in enumerate(order):
                        lo, hi = max(0, 1 - dw), min(W, W + 1 - dw)
                        src = dims(in_, a * shift + lo + dw - 1, (stride, rows), (1, hi - lo))
                        dst = out_.rearrange("p (r w) -> p r w", w=W)[:, :, lo:hi]
                        last = nc.tensor.matmul(dst, band_[:, a * 3 + dw, :], src, start=(number == 0),
                                                stop=(number == 8), skip_group_check=True)
                last.then_inc(unit_mm, 1)

            pe.wait_ge(consts_in, CONSTS)
            pe.wait_ge(dve_init, 1)

            def step1(b, i, first, last):
                n = at(b, i)
                if lagged(i, 2, first, last):
                    j, m = (i - 2) % STEPS, at(b, i - 2)
                    slot = j % SLOTS
                    pe.wait_ge(v_up, m + 1)
                    for gr in range(NGRP):
                        if not (first and i == 2 and gr < 2):
                            pe.wait_ge(vt_up, m * NGRP + gr - 1)
                        for k in range(PER * gr, min(NBLK, PER * gr + PER)):
                            at_ = gr % 2 * 1024 + (k - PER * gr) * P
                            ins = nc.tensor.transpose(dims(PS[:, :, :], at_, (1, P))[0:BLK], blocks(slot, k), IDN)
                        ins.then_inc(transposed, 1)
                    if not (first and i == 2):
                        pe.wait_ge(sums_out, 3 * m)
                    for k in range(NBLK):
                        ins = nc.tensor.matmul(PS[0:BLK, SUMS, CCOL + k:CCOL + k + 1], blocks(slot, k), ONES[:, 0:1],
                                               start=True, stop=True)
                    ins.then_inc(c_summed, 1)
                    pe.wait_ge(vt_up, (m + 1) * NGRP)
                    for k in range(NBLK):
                        hb, o = k // NO, k % NO
                        dst = dims(PS[:, :, :], SUMS * 512 + RB * hb, (HCOL + CQ * o - RB * hb, 2), (1, RB))
                        ins = nc.tensor.matmul(dst, VT[0:BLK, j % 2, k, :],
                                               WH[0:BLK].rearrange("p (a b) -> p a b", a=2),
                                               start=(k == 0), stop=(k == NBLK - 1), skip_group_check=True)
                    ins.then_inc(hw_summed, 1)
                if not last:
                    par = i % 2
                    pe.wait_ge(summed, n + 1)
                    if not (first and i == 0):
                        pe.wait_ge(sigma, n)
                    nc.tensor.matmul(PS[:, STAT, 0:1], GRP[:, 0, :], SUM[:, par:par + 1], start=True, stop=True)
                    nc.tensor.matmul(PS[:, STAT, 1:2], GRP[:, 1, :], SUM[:, par:par + 1], start=True,
                                     stop=True).then_inc(mean_mm, 1)
                mine = here(i) if not first else []
                if mine and i == here_first:
                    pe.wait_ge(bands_up, 1)
                for q, kind, u in mine[:1]:
                    unit(b - 1, q, kind, u)
                if not last:
                    pe.wait_ge(e_up, n + 1)
                    nc.tensor.matmul(PS[:, STAT, 2:3], GRP[:, 2, :], ER[:, par:par + 1], start=True,
                                     stop=True).then_inc(var_mm, 1)
                for q, kind, u in mine[1:]:
                    unit(b - 1, q, kind, u)

            here_first = unit_step[0]
            run(pe, step1)

            pe.wait_ge(fin_up, 1)
            nc.tensor.matmul(PS[:, STAT, 0:16], ONES, FIN.rearrange("p a b -> p (a b)"), start=True,
                             stop=True).then_inc(fin_mm, 1)
            pe.wait_ge(fin_up, 2)
            nc.tensor.matmul(PS[:, STAT, 16:24], ONES, FD.rearrange("p a b -> p (a b)"), start=True,
                             stop=True).then_inc(fin_mm, 1)
            pe.wait_ge(sel_up, 1)

            def step2(b, i, first, last):
                if lagged(i, 8, first, last):
                    j, m = (i - 8) % STEPS, at(b, i - 8)
                    e = b if i >= 8 else b - 1
                    g, t = j // T, j % T
                    pe.wait_ge(pool, 9 * (e * HALVES + g + 1))
                    if not (first and i == 8):
                        pe.wait_ge(gt_up, m)
                    for s in range(3):
                        at_ = (t % 4 * 2 + t // 4) * TEAR
                        ins = nc.tensor.transpose(PS[0:TEAR, 7, s * P // 2:(s + 1) * P // 2].bitcast(BF16),
                                                  G34P[:, g, s, at_:at_ + TEAR], IDB)
                    ins.then_inc(gt_mm, 1)
                if lagged(i, 9, first, last):
                    j, m = (i - 9) % STEPS, at(b, i - 9)
                    e = b if i >= 9 else b - 1
                    g = j // T
                    pe.wait_ge(gt_up, m + 1)
                    pe.wait_ge(row_in[j % 2], (e * (STEPS // 2) + j // 2 + 1) * 16)
                    for gr in range(G2):
                        if not (first and i == 9 and gr < 2):
                            pe.wait_ge(a_up, m * G2 + gr - 1)
                        for ch in range(3 * gr, min(CHUNKS, 3 * gr + 3)):
                            dst = PS[:, (3 * j + gr) % 2 * 3 + ch - 3 * gr, 0:CH]
                            cols = slice(ch * CH, (ch + 1) * CH)
                            for s in range(3):
                                k = TEAR + 3 if s == 0 else TEAR
                                nc.tensor.matmul(dst, GT[0:k, j % 2, s, :], SELR[0:k, j % 2, cols], start=(s == 0),
                                                 stop=False)
                            for s in range(3):
                                ins = nc.tensor.matmul(dst, IDB, G2P[:, g, s, cols], start=False, stop=(s == 2))
                        ins.then_inc(gates_mm, 1)

            run(pe, step2)


def constants(B):
    f = np.float32
    eye = np.eye(P)
    blockdiag = np.kron(np.eye(P // GROUP), np.ones((GROUP, GROUP))) / GROUP
    sq = np.stack([eye, -blockdiag / HW, (blockdiag - eye) / HW, blockdiag], 1)
    wh = np.zeros((BLK, 2, RB))
    for h in range(RB):
        for q in range(CQ):
            wh[h * CQ + q, 0, h] = wh[h * CQ + q, 1, q] = 1
    mask = np.zeros((CIN, 4, 3, CT))
    for d in range(3):
        for c in range(CT):
            mask[c + d, :, d, c] = 1
    mask1 = np.zeros((2, H, 3, H))
    for d in range(3):
        for h in range(H):
            if 0 <= h + d - 1 < H:
                mask1[:, h + d - 1, d, h] = 1
    kind = np.zeros((P, 8))
    q = np.arange(P)
    first = q % 4 < 2
    kind[:, 0], kind[:, 1], kind[:, 2] = first, ~first / T, ~first / H
    kind[:, 3], kind[:, 4] = q % 2 == 0, q % 2 == 1
    kind[:, 5], kind[:, 6] = q < H, (q >= H) / (P * HALVES)
    gate = np.zeros((P, 24))
    weight = gate[:, 0:16].reshape(P, 4, 2, 2)
    weight[:, 0, 0] = 1 / H
    weight[:, 1:, 0] = CT * (NCT - 1) / (P * HALVES) / MOUT
    weight[:, 1:, 1] = (MLAST // 4) / (P * HALVES) / MLAST
    gate[:, 0:16] = weight.reshape(P, 16)
    valid = np.zeros((P, 4, 2))
    valid[:, 0, 0] = q < H
    valid[:, 1:, 0] = (q < MOUT)[:, None]
    valid[:, 1:, 1] = (q < MLAST)[:, None]
    gate[:, 16:] = valid.reshape(P, 8)
    sel = np.zeros((2, W, H, W))
    for a in range(W):
        sel[0, a, :, a] = 1
        sel[1, a, a, :] = 1
    return [("k_sq", sq.astype(f)), ("k_wh", wh.reshape(BLK, -1).astype(f)), ("k_mask", mask.reshape(KIN, 3, CT).astype(f)),
            ("k_mask1", mask1.reshape(2 * H, 3, H).astype(f)), ("k_kind", kind.astype(f)), ("k_gate", gate.astype(f)),
            ("k_sel", sel.reshape(TEAR, HW).astype(f))]


def kernel(x, L0_conv_w_str, L0_conv_w_sr, L0_conv_w_trh, L0_conv_w_trw, L0_conv_gamma, L0_conv_beta):
    from concourse import bacc
    from concourse.bass_utils import run_bass_kernel_spmd

    arrays = [("x", x), ("w_str", L0_conv_w_str), ("w_sr", L0_conv_w_sr), ("w_trh", L0_conv_w_trh),
              ("w_trw", L0_conv_w_trw), ("gamma", L0_conv_gamma), ("beta", L0_conv_beta)]
    arrays += constants(x.shape[0] // T)
    nc = bacc.Bacc("TRN2", target_bir_lowering=False, num_devices=1)
    feed, args = {}, []
    for name, a in arrays:
        a = np.ascontiguousarray(a)
        feed[name] = a
        args.append(nc.dram_tensor(name, a.shape, mybir.dt.from_np(a.dtype), kind="ExternalInput").ap())
    out = nc.dram_tensor("out", x.shape, F32, kind="ExternalOutput").ap()
    build(nc, *args, out)
    r = run_bass_kernel_spmd(nc, [feed], core_ids=[0])
    return r.results[0]["out"]
```

```python
from contextlib import ExitStack

import numpy as np

import concourse.bass as bass
from concourse import mybir

F32 = mybir.dt.float32
BF16 = mybir.dt.bfloat16
ALU = mybir.AluOpType
ACT = mybir.ActivationFunctionType
AX = mybir.AxisListType

P = 128
T = 8
HALVES = 2
STEPS = HALVES * T
GROUP = 8
H = W = 56
HW = H * W
EPS_ = 1e-5
SLOTS = 4

CT = 29
NCT = -(-P * HALVES // CT)
CIN = CT + 2
KIN = CIN * 4
MOUT = CT * 4
MLAST = 4 * (P * HALVES - CT * (NCT - 1))
CPAD = CT * NCT + 2
PL2 = (H // 2 + 1) * W
PL34 = (T // 2 + 1) * W
ROW2 = 4 * PL2
ROW34 = 4 * 2 * PL34
ODD = PL2 + W
N2 = H // 4 // 2 * W
IN2 = (H // 4 + 1) * W
N34 = T // 4 * W
UNITS2 = 2 * NCT
RING2, RING34, RING1 = 2, 3, 2
RING = {"2": RING2, "34": RING34, "1": RING1}
RB, CQ = 28, 4
NHB, NO = H // RB, W // CQ
BLK = RB * CQ
NBLK = NHB * NO
PER = NO // 2
NGRP = NBLK // PER
CH = 8 * W
CHUNKS = HW // CH
CSR = T * CHUNKS
G2 = -(-CHUNKS // 3)
TEAR = H * 2


def dims(base, offset, *pairs):
    return bass.AP(tensor=base.tensor, offset=base.offset + offset, ap=[list(base.ap[0])] + [list(p) for p in pairs])


def units_of_entry():
    u2, u34 = [("2", u) for u in range(UNITS2)], [("34", u) for u in range(NCT)]
    units = []
    while u2 or u34:
        units += u2[:2] + u34[:1]
        u2, u34 = u2[2:], u34[1:]
    units = units[:3] + [("t", 0)] + units[3:] + [("1", 0), ("1", 1)]
    first, n = 3, STEPS - 3
    steps = [first + q * n // len(units) for q in range(len(units))]
    assert all(steps.count(i) <= 3 for i in steps) and steps.count(STEPS - 1) <= 2
    return units, steps


def build(nc, x, w_str, w_sr, w_trh, w_trw, gamma, beta, k_sq, k_mask, k_mask1, k_kind, k_gate, k_sel, out):
    B = x.shape[0] // T
    xt = x.rearrange("(b t) (g c) h w -> b g t c (h w)", t=T, c=P)
    ot = out.rearrange("(b t) (g c) h w -> b g t c (h w)", t=T, c=P)
    ZC = B * T * HW // P
    units, unit_step = units_of_entry()
    NU = len(units)
    counted = [q for q in range(NU) if units[q][0] != "t"]

    ctx = ExitStack()
    with ctx:
        def sem(name):
            return ctx.enter_context(nc.semaphore(name))

        p2_d = nc.dram_tensor("p2_d", [B, CPAD, ROW2], F32)
        p34_d = nc.dram_tensor("p34_d", [B, CPAD, ROW34], F32)
        p1_d = nc.dram_tensor("p1_d", [B, NHB, T + 2, HW // NHB], F32)
        s1_d = nc.dram_tensor("s1_d", [B, T + 2, HW], F32)
        z2_d = nc.dram_tensor("z2_d", [B, CT * NCT, HW], F32)
        z34_d = nc.dram_tensor("z34_d", [B, CT * NCT, T * 2 * W], F32)
        z1_d = nc.dram_tensor("z1_d", [B, T, H, W], F32)
        g1_d = nc.dram_tensor("g1_d", [3, B * T * HW], BF16)
        st_d = nc.dram_tensor("st_d", [B, HALVES, P, 2 * T], F32)

        words = 212800 // 4
        S = ctx.enter_context(nc.sbuf_tensor("S", [P, words], F32))

        def taker(at, end):
            place = [at]

            def take(*shape, dt=F32):
                n = int(np.prod(shape))
                n = n if dt == F32 else n // 2
                at = (place[0] + 7) // 8 * 8
                place[0] = at + n
                assert at + n <= end, (at + n, end)
                v = S[:, at:at + n]
                if dt != F32:
                    v = v.bitcast(dt)
                if len(shape) > 1:
                    names = "abcdef"[:len(shape)]
                    v = v.rearrange(f"p ({' '.join(names)}) -> p {' '.join(names)}", **dict(zip(names, shape)))
                return v
            return take, place

        take, used = taker(0, words)
        V = take(SLOTS, HW)
        IDN = take(P)
        GRP = take(3, P)
        ONES = take(P)
        EPS = take(1)
        CONST = take(2)
        GB = take(8)
        KG = take(24)
        S2 = take(B, UNITS2, 6)
        S34 = take(2, B, NCT, 6)
        S1 = take(B, HALVES, 6)
        FIN = take(4, 4)
        FT = take(4, 4)
        FM = take(4, 2)
        FD = take(4, 2)
        FV = take(4)
        SCL = take(2, 4)
        common_end = used[0]
        ACC = take(HALVES, 2, 2 * PL2)
        HT = take(HW // 2)
        JUNK = take(HW, dt=BF16)
        P34 = take(HALVES, 8, PL34)
        IN2B = take(RING2, IN2)
        IN34B = take(RING34, 2 * PL34)
        IN1B = take(2, (T // 2 + 2) * W)
        CM = take(HALVES, T * NBLK)
        CB = take(T * NBLK)
        CS = take(CH)
        PICK = take(2 * CSR - 1)
        Z2B = take(RING2, N2)
        Z34B = take(RING34, 2 * N34)
        Z1B = take(2, T // 2 * W)
        P1T = Z1B.rearrange("p a n -> p (a n)")
        BAND = take(3, 9, MOUT)
        BAND1 = take(9, H)
        RM = take(HALVES, 2, T)
        SUM = take(2)
        CEN = take(2)
        SQ = take(2)
        ER = take(2)
        SG = take(2)
        NMR = take(2)
        MD = take(2, 2)
        phase1_end = used[0]
        take3, _ = taker(IN2B.offset, IN2B.offset + RING2 * IN2)
        MASK = take3(3, CT)
        MASK1 = take3(3, H)
        KIND = take3(8)
        WB = take3(4, 54)
        WK = take3(27)
        R9 = take3(3, 9, 3)
        RP = take3(3, 8, 3)
        TMP = take3(9 * H)
        take2, _ = taker(common_end, phase1_end)
        AB = take2(2, HW)
        G2Z = take2(HW)
        G2F = take2(HW)
        G2P = take2(2, 3, HW, dt=BF16)
        SELR = take2(2, HW, dt=BF16)
        G34Z = take2(T * 2 * W)
        G34F = take2(T * 2 * W)
        G34P = take2(2, 3, T * 2 * W, dt=BF16)
        GT = take2(2, 3, P, dt=BF16)
        IDB = take2(P, dt=BF16)
        RM2 = take2(2, 2, T)
        R4 = take2(2, T)
        take4, _ = taker(AB.offset, AB.offset + 2 * HW)
        Z1F = take4(ZC)
        Z1P = take4(3, ZC, dt=BF16)

        PS = ctx.enter_context(nc.psum_tensor("PS", [P, 8, 512], F32))
        SUMS, STAT, CONV = 4, 5, 6

        consts_in = sem("consts_in")
        x_in = [sem(f"x_in{i}") for i in range(SLOTS)]
        zeros_up = sem("zeros_up")
        pads_out = sem("pads_out")
        pool_init = sem("pool_init")
        dve_init = sem("dve_init")
        chain = sem("chain")
        bands_up = sem("bands_up")
        summed = sem("summed")
        centred = sem("centred")
        squared = sem("squared")
        mean_mm = sem("mean_mm")
        md_copied = sem("md_copied")
        e_up = sem("e_up")
        var_mm = sem("var_mm")
        sigma = sem("sigma")
        r_up = sem("r_up")
        rm_up = sem("rm_up")
        v_up = sem("v_up")
        transposed = sem("transposed")
        c_summed = sem("c_summed")
        cs_up = sem("cs_up")
        maxed = sem("maxed")
        t_summed = sem("t_summed")
        h_tree = sem("h_tree")
        c_maxed = sem("c_maxed")
        cb_up = sem("cb_up")
        p2_out = [sem(f"p2_out{g}") for g in range(HALVES)]
        p34_out = [sem(f"p34_out{g}") for g in range(HALVES)]
        st_out = [sem(f"st_out{g}") for g in range(HALVES)]
        in2 = [sem(f"in2_{i}") for i in range(RING2)]
        in34 = [sem(f"in34_{i}") for i in range(RING34)]
        in1 = [sem(f"in1_{i}") for i in range(2)]
        unit_mm = sem("unit_mm")
        unit_out = sem("unit_out")
        unit_stat = sem("unit_stat")
        z2_out = [sem(f"z2_out{i}") for i in range(RING2)]
        z34_out = [sem(f"z34_out{i}") for i in range(RING34)]
        z1_out = [sem(f"z1_out{i}") for i in range(2)]
        p1_out = sem("p1_out")
        s1_out = sem("s1_out")
        fin_up = sem("fin_up")
        fin_mm = sem("fin_mm")
        fin_sg = sem("fin_sg")
        scl_up = sem("scl_up")
        sel_in = sem("sel_in")
        sel_up = sem("sel_up")
        z1_in = sem("z1_in")
        g1_up = sem("g1_up")
        g1_split = sem("g1_split")
        g1_out = sem("g1_out")
        z2_in = sem("z2_in")
        z34_in = sem("z34_in")
        rm_in = sem("rm_in")
        g2_up = sem("g2_up")
        g34_up = sem("g34_up")
        pool = sem("pool")
        row_in = [sem(f"row_in{i}") for i in range(2)]
        y_in = [sem(f"y_in{i}") for i in range(SLOTS)]
        gt_mm = sem("gt_mm")
        gt_up = sem("gt_up")
        gates_mm = sem("gates_mm")
        a_up = sem("a_up")
        scaled = sem("scaled")
        done = sem("done")
        y_out = [sem(f"y_out{i}") for i in range(SLOTS)]

        CONSTS = 16 * 12
        PADS = 16 * (2 * (1 + B) + 4)

        def at(b, i):
            return b * STEPS + i

        def later(e):
            return not isinstance(e, int) or e > 0

        def lagged(i, lag, first, last):
            return not (first and i < lag) and not (last and i >= lag)

        def run(eng, step):
            for i in range(STEPS):
                step(0, i, True, False)
            with eng.Fori(1, B) as b:
                for i in range(STEPS):
                    step(b, i, False, False)
            for i in range(STEPS):
                step(B, i, False, True)

        def here(i):
            return [(q, *units[q]) for q in range(NU) if unit_step[q] == i]

        def placed(i, k):
            return here(i)[k:k + 1]

        def late(i):
            return placed(i - 1, 2) if i else []

        def q_of(kind, u):
            return units.index((kind, u))

        def frame_slot(t):
            return t % 2, (t + 1) // 2

        def pooled(g, kind, t, branch):
            p, q = frame_slot(t)
            return P34[:, g, (kind * 2 + p) * 2 + branch, q * W:(q + 1) * W]

        def plane(g, kind):
            return dims(ACC, (g * 2 + kind) * 2 * PL2, (ODD, 2), (W, H // 2), (1, W))

        def tile_rows(slot):
            return V[:, slot, :].rearrange("p (q e w) -> p e q w", e=2, w=W)

        def blocks(slot, k):
            return dims(V[:, slot, :], k // NO * RB * W + k % NO, (NO, BLK))

        def over_c(g, t, k):
            return dims(CM, (g * T + t // 4 * 4) * NBLK + (k // NO * 4 + t % 4) * NO + k % NO, (1, PER))

        block = ctx.enter_context(nc.Block())

        @block.sync
        def _(sp):
            small = [(IDN, k_sq[:, 0, :]), (GRP, k_sq[:, 1:4, :]), (MASK[0:KIN], k_mask),
                     (MASK1[0:2 * H], k_mask1), (KIND, k_kind),
                     (KG, k_gate),
                     (GB[:, 0:4], gamma.rearrange("(o n) -> o n", o=1).broadcast_to([P, 4])),
                     (GB[:, 4:8], beta.rearrange("(o n) -> o n", o=1).broadcast_to([P, 4]))]
            small += [(WB[:, i, :], w.rearrange("o k a b c -> o (k a b c)").broadcast_to([P, 54]))
                      for i, w in enumerate((w_str, w_sr, w_trh, w_trw))]

            def pads():
                zero = ACC[:, 1].rearrange("p k n -> p (k n)")
                sp.wait_ge(zeros_up, 1)
                for d, n in ((p2_d, ROW2), (p34_d, ROW34)):
                    sp.dma_start(d[:, 0, :], zero[0:B, 0:n]).then_inc(pads_out, 16)
                    for b in range(B):
                        sp.dma_start(d[b, P * HALVES + 1:CPAD, :],
                                     zero[0:CPAD - P * HALVES - 1, 0:n]).then_inc(pads_out, 16)
                for tt in (0, T + 1):
                    sp.dma_start(p1_d[:, :, tt, :].rearrange("b h n -> (b h) n"),
                                 zero[0:NHB * B, 0:HW // NHB]).then_inc(pads_out, 16)
                    sp.dma_start(s1_d[:, tt, :], zero[0:B, 0:HW]).then_inc(pads_out, 16)

            def unit_in(e, kind, u):
                if kind == "t":
                    return
                ring = RING[kind]
                if u >= ring:
                    sp.wait_ge(unit_mm, e * NU + q_of(kind, u - ring) + 1)
                if kind == "2":
                    ct, kc = u // 2, u % 2
                    rows = p2_d[e, CT * ct:CT * ct + CIN, :].rearrange("c (k n) -> (c k) n", k=4)
                    sp.dma_start(IN2B[0:KIN, u % RING2, :], rows[:, kc * 2 * N2:kc * 2 * N2 + IN2]).then_inc(in2[u % RING2], 16)
                elif kind == "34":
                    rows = p34_d[e, CT * u:CT * u + CIN, :].rearrange("c (k n) -> (c k) n", k=4)
                    sp.dma_start(IN34B[0:KIN, u % RING34, :], rows).then_inc(in34[u % RING34], 16)
                else:
                    sp.wait_ge(p1_out, (e + 1) * 64)
                    sp.wait_ge(s1_out, (e + 1) * 16)
                    for hb in (1, 0):
                        rows = p1_d[e, hb, T // 2 * u:T // 2 * u + T // 2 + 2, :].rearrange(
                            "t (o h q) -> h (t o) q", o=NO, q=CQ)
                        sp.dma_start(IN1B[RB * hb:RB * (hb + 1), u, :].rearrange("h (n q) -> h n q", q=CQ),
                                     rows).then_inc(in1[u], 16)
                    rows = s1_d[e, T // 2 * u:T // 2 * u + T // 2 + 2, :].rearrange("t (h w) -> h t w", w=W)
                    sp.dma_start(IN1B[H:2 * H, u, :].rearrange("h (t w) -> h t w", w=W), rows).then_inc(in1[u], 16)

            def unit_store(e, q, kind, u):
                sp.wait_ge(unit_out, e * NU + q + 1)
                if kind == "2":
                    ct, kc = u // 2, u % 2
                    rows = z2_d[e, CT * ct:CT * (ct + 1), :].rearrange("c (j n) -> (c j) n", j=4)
                    sp.dma_start(rows[:, kc * N2:(kc + 1) * N2], Z2B[0:MOUT, u % RING2, :]).then_inc(z2_out[u % RING2], 16)
                elif kind == "34":
                    rows = z34_d[e, CT * u:CT * (u + 1), :].rearrange("c (j n) -> (c j) n", j=4)
                    sp.dma_start(rows, Z34B[0:MOUT, u % RING34, :]).then_inc(z34_out[u % RING34], 16)
                elif kind == "1":
                    sp.dma_start(z1_d[e, T // 2 * u:T // 2 * (u + 1)].rearrange("t h w -> h t w"),
                                 Z1B[0:H, u, :].rearrange("h (t w) -> h t w", w=W)).then_inc(z1_out[u], 16)
                else:
                    m = T // 2 * NO
                    for th in range(2):
                        for hb in range(NHB):
                            rows = p1_d[e, hb, 1 + T // 2 * th:1 + T // 2 * (th + 1), :].rearrange(
                                "t (o n) -> (t o) n", o=NO)
                            src = P1T[hb * m:(hb + 1) * m, th * BLK:(th + 1) * BLK]
                            sp.dma_start(rows, src).then_inc(p1_out, 16)

            def step1(b, i, first, last):
                if not last:
                    slot, g, t, n = i % SLOTS, i // T, i % T, at(b, i)
                    if not (first and i < SLOTS):
                        sp.wait_ge(h_tree, 7 * (n - SLOTS + 1))
                        sp.wait_ge(maxed, n - SLOTS + 1)
                        sp.wait_ge(t_summed, n - SLOTS + 1)
                        sp.wait_ge(c_summed, n - SLOTS + 1)
                    sp.dma_start(V[:, slot, :], xt[b, g, t]).then_inc(x_in[slot], 16)
                if first and i == 0:
                    for dst, src in small:
                        sp.dma_start(dst, src).then_inc(consts_in, 16)
                if first and i == 2:
                    pads()
                g = {T + 2: 0, 2: 1}.get(i)
                if (g == 0 and not last) or (g == 1 and not first):
                    e = b if g == 0 else b - 1
                    n = at(e, T * (g + 1))
                    sp.wait_ge(h_tree, 7 * n)
                    sp.wait_ge(maxed, n)
                    sp.wait_ge(t_summed, n)
                    sp.wait_ge(rm_up, n)
                    sp.dma_start(p2_d[e, 1 + P * g:1 + P * (g + 1), :],
                                 ACC[:, g].rearrange("p k n -> p (k n)")).then_inc(p2_out[g], 16)
                    sp.dma_start(p34_d[e, 1 + P * g:1 + P * (g + 1), :],
                                 P34[:, g].rearrange("p k n -> p (k n)")).then_inc(p34_out[g], 16)
                    sp.dma_start(st_d[e, g], RM[:, g].rearrange("p a n -> p (a n)")).then_inc(st_out[g], 16)
                if first:
                    return
                e = b - 1
                if i == 3:
                    sp.wait_ge(pads_out, PADS)
                    for g in range(HALVES):
                        sp.wait_ge(p2_out[g], (e + 1) * 16)
                        sp.wait_ge(p34_out[g], (e + 1) * 16)
                if i == 3:
                    sp.wait_ge(cs_up, e + 1)
                    sp.dma_start(s1_d[e, 1:T + 1, :].rearrange("t (r n) -> (t r) n", n=CH),
                                 CS[0:CSR]).then_inc(s1_out, 16)
                if i:
                    for q, kind, u in here(i - 1):
                        unit_store(e, q, kind, u)
                for q, kind, u in here(i):
                    unit_in(e, kind, u)
                if i == STEPS - 1:
                    for q, kind, u in here(i):
                        unit_store(e, q, kind, u)

            run(sp, step1)

            for s in z2_out:
                sp.wait_ge(s, 16 * B * UNITS2 // RING2)
            for s in z34_out:
                sp.wait_ge(s, 16 * B * NCT // RING34)
            for s in z1_out:
                sp.wait_ge(s, 16 * B)
            for g in range(HALVES):
                sp.wait_ge(st_out[g], 16 * B)
            sp.wait_ge(unit_stat, B * len(counted))
            sp.wait_ge(unit_mm, B * NU)
            sp.wait_ge(c_maxed, B * STEPS * NGRP)
            sp.wait_ge(p1_out, B * 64)
            sp.wait_ge(s1_out, B * 16)
            sp.dma_start(G2F[0:TEAR, :], k_sel).then_inc(sel_in, 16)
            sp.dma_start(Z1F, z1_d.rearrange("b t h w -> (b t h w)").rearrange("(p n) -> p n", p=P)).then_inc(z1_in, 16)
            g1_rows = g1_d.rearrange("s (n c) -> n s c", c=HW)

            def step2(b, i, first, last):
                n, g, t = at(b, i), i // T, i % T
                if not last and t == 0:
                    if later(b) or g:
                        sp.wait_ge(pool, 9 * (b * HALVES + g))
                    sp.dma_start(G2Z, z2_d[b, P * g:P * (g + 1), :]).then_inc(z2_in, 16)
                    sp.dma_start(G34Z, z34_d[b, P * g:P * (g + 1), :]).then_inc(z34_in, 16)
                if not last and t == 2:
                    if not first:
                        sp.wait_ge(done, n - 10)
                    sp.dma_start(RM2[:, g].rearrange("p a n -> p (a n)"), st_d[b, g]).then_inc(rm_in, 16)
                if lagged(i, 10, first, last):
                    j = (i - 10) % STEPS
                    e = b if i >= 10 else b - 1
                    sp.wait_ge(done, n - 9)
                    sp.dma_start(ot[e, j // T, j % T], V[:, j % SLOTS, :]).then_inc(y_out[j % SLOTS], 16)
                if first and i == 8:
                    sp.wait_ge(g1_split, 1)
                    for s in range(3):
                        sp.dma_start(g1_d[s].rearrange("(p n) -> p n", p=P), Z1P[:, s, :]).then_inc(g1_out, 16)
                    sp.wait_ge(g1_out, 48)
                    sp.wait_ge(sel_up, 1)
                if lagged(i, 8, first, last):
                    j = (i - 8) % STEPS
                    e = b if i >= 8 else b - 1
                    if not (first and i < 10):
                        sp.wait_ge(gates_mm, (n - 9) * G2)
                    sp.dma_start(SELR[TEAR:TEAR + 3, j % 2, :], g1_rows[e * T + j % T]).then_inc(row_in[j % 2], 16)
                if lagged(i, 7, first, last):
                    j = (i - 7) % STEPS
                    e = b if i >= 7 else b - 1
                    if not (first and i < 11):
                        sp.wait_ge(y_out[j % SLOTS], (e * (STEPS // SLOTS) + j // SLOTS) * 16)
                    sp.dma_start(V[:, j % SLOTS, :], xt[e, j // T, j % T]).then_inc(y_in[j % SLOTS], 16)

            run(sp, step2)
            for s in y_out:
                sp.wait_ge(s, 16 * B * STEPS // SLOTS)

        @block.gpsimd
        def _(eng):
            nc.gpsimd.memset(ACC.rearrange("p a b n -> p (a b n)"), 0.0).then_inc(zeros_up, 1)
            nc.gpsimd.memset(CONST[:, 0:1], 0.0).then_inc(pool_init, 1)
            nc.gpsimd.memset(CONST[:, 1:2], 0.25).then_inc(pool_init, 1)
            eng.wait_ge(pool_init, 2)

            def step1(b, i, first, last):
                if not lagged(i, 2, first, last):
                    return
                j, n = (i - 2) % STEPS, at(b, i - 2)
                g, t = j // T, j % T
                v = V[:, j % SLOTS, :]
                k = 7 * n
                eng.wait_ge(v_up, n + 1)
                if not (first and i == 2):
                    eng.wait_ge(h_tree, k)
                nc.gpsimd.tensor_tensor(HT, v[:, 0:HW // 2], v[:, HW // 2:HW], ALU.add).then_inc(h_tree, 1)
                if t == 0:
                    if not first:
                        eng.wait_ge(p2_out[g], b * 16)
                        eng.wait_ge(p34_out[g], b * 16)
                    elif g:
                        eng.wait_ge(pads_out, PADS)
                    else:
                        eng.wait_ge(zeros_up, 1)
                    nc.gpsimd.tensor_tensor(plane(g, 1), tile_rows(j % SLOTS),
                                            dims(CONST, 0, (0, 2), (0, H // 2), (0, W)), ALU.add).then_inc(t_summed, 1)
                else:
                    eng.wait_ge(t_summed, n)
                    nc.gpsimd.tensor_tensor(plane(g, 1), plane(g, 1), tile_rows(j % SLOTS),
                                            ALU.add).then_inc(t_summed, 1)
                for rows in (14, 7, 3):
                    k = k + 1
                    eng.wait_ge(h_tree, k)
                    nc.gpsimd.tensor_tensor(HT[:, 0:rows * W], HT[:, 0:rows * W], HT[:, rows * W:2 * rows * W],
                                            ALU.add).then_inc(h_tree, 1)
                k = k + 1
                eng.wait_ge(h_tree, k)
                nc.gpsimd.tensor_tensor(HT[:, 0:W], HT[:, 0:W], HT[:, 6 * W:7 * W], ALU.add).then_inc(h_tree, 1)
                nc.gpsimd.tensor_tensor(HT[:, W:2 * W], HT[:, W:2 * W], HT[:, 2 * W:3 * W], ALU.add).then_inc(h_tree, 1)
                eng.wait_ge(h_tree, k + 2)
                nc.gpsimd.tensor_tensor(pooled(g, 1, t, 0), HT[:, 0:W], HT[:, W:2 * W], ALU.add).then_inc(h_tree, 1)

            run(eng, step1)

            def step2(b, i, first, last):
                g, t = i // T, i % T
                if last or t != 4:
                    return
                e, n = b * HALVES + g, at(b, i)
                if not first:
                    eng.wait_ge(gates_mm, (n - 12) * G2)
                    eng.wait_ge(a_up, (n - 12) * G2)
                eng.wait_ge(g2_up, e + 1)
                eng.wait_ge(g34_up, e + 1)
                k = 9 * e
                for full, rest, parts in ((G2F, G2Z, G2P[:, g]), (G34F, G34Z, G34P[:, g])):
                    zero = dims(CONST, 0, (0, full.shape[-1]))
                    nc.gpsimd.tensor_tensor(parts[:, 0, :], full, zero, ALU.add).then_inc(pool, 1)
                    eng.wait_ge(pool, k + 1)
                    nc.gpsimd.tensor_tensor(rest, full, parts[:, 0, :], ALU.subtract).then_inc(pool, 1)
                    eng.wait_ge(pool, k + 2)
                    nc.gpsimd.tensor_tensor(parts[:, 1, :], rest, zero, ALU.add).then_inc(pool, 1)
                    eng.wait_ge(pool, k + 3)
                    nc.gpsimd.tensor_tensor(parts[:, 2, :], rest, parts[:, 1, :], ALU.subtract).then_inc(pool, 1)
                    k = k + 4
                eng.wait_ge(rm_in, (e + 1) * 16)
                nc.gpsimd.tensor_tensor(R4[:, g, :], RM2[:, g, 1, :], dims(CONST, 1, (0, T)), ALU.mult).then_inc(pool, 1)

            run(eng, step2)

        @block.scalar
        def _(act):
            def unit(e, q, kind, u):
                act.wait_ge(unit_mm, e * NU + q + 1)
                src = PS[:, CONV + q % 2, :]
                if kind == "t":
                    for s in z1_out:
                        act.wait_ge(s, e * 16)
                    act.wait_ge(unit_stat, e * len(counted))
                    nc.scalar.copy(P1T[0:BLK, 0:2 * BLK], src[0:BLK, 0:2 * BLK]).then_inc(unit_out, 1)
                    return
                ring = RING[kind]
                outs = {"2": z2_out, "34": z34_out, "1": z1_out}[kind]
                per = {"2": UNITS2, "34": NCT, "1": 2}[kind] // ring
                act.wait_ge(outs[u % ring], (e * per + u // ring) * 16)
                before = counted.index(q_of(kind, u - ring)) + 1 if u >= ring else 0
                act.wait_ge(unit_stat, e * len(counted) + before)
                dst, m, width = {"2": (Z2B, MOUT, N2), "34": (Z34B, MOUT, 2 * N34), "1": (Z1B, H, T // 2 * W)}[kind]
                dst, src = dst[0:m, u % ring, :], src[0:m, 0:width]
                if kind == "1":
                    dst = dst.rearrange("p (t q o) -> p t o q", q=CQ, o=NO)
                    src = src.rearrange("p (t o q) -> p t o q", q=CQ, o=NO)
                nc.scalar.copy(dst, src).then_inc(unit_out, 1)

            act.wait_ge(dve_init, 1)

            def step1(b, i, first, last):
                n = at(b, i)
                if i == 2 and not first:
                    act.wait_ge(c_summed, at(b, 0))
                    if later(b - 1):
                        act.wait_ge(s1_out, (b - 1) * 16)
                    nc.scalar.copy(CS[0:CSR].rearrange("p (h o q) -> p h q o", o=NO, q=CQ),
                                   PS[0:CSR, SUMS, 0:CH].rearrange("p (h q o) -> p h q o", o=NO, q=CQ)).then_inc(cs_up, 1)
                if lagged(i, 1, first, last):
                    j = (i - 1) % STEPS
                    act.wait_ge(rm_up, n)
                    v = V[:, j % SLOTS, :]
                    nc.scalar.activation(v, v, ACT.Identity, scale=RM[:, j // T, 1, j % T:j % T + 1],
                                         bias=NMR[:, j % 2:j % 2 + 1]).then_inc(v_up, 1)
                if not last:
                    slot, par = i % SLOTS, i % 2
                    act.wait_ge(x_in[slot], (b * (STEPS // SLOTS) + i // SLOTS + 1) * 16)
                    if not (first and i == 0):
                        act.wait_ge(squared, n)
                    nc.scalar.activation(JUNK, V[:, slot, :], ACT.Copy,
                                         accum_out=SUM[:, par:par + 1]).then_inc(summed, 1)
                    act.wait_ge(summed, n + 1)
                    nc.scalar.mul(CEN[:, par:par + 1], SUM[:, par:par + 1], -1.0 / (HW * W)).then_inc(centred, 1)
                if not first:
                    for q, kind, u in late(i):
                        unit(b - 1, q, kind, u)
                if not last:
                    act.wait_ge(centred, n + 1)
                    nc.scalar.activation(JUNK, V[:, slot, :], ACT.Square, scale=1.0 / W, bias=CEN[:, par:par + 1],
                                         accum_out=SQ[:, par:par + 1]).then_inc(squared, 1)
                if not first:
                    for q, kind, u in placed(i, 0):
                        unit(b - 1, q, kind, u)
                if not last:
                    act.wait_ge(var_mm, n + 1)
                    nc.scalar.activation(SG[:, par:par + 1], PS[:, STAT, 2:3], ACT.Sqrt, bias=EPS).then_inc(sigma, 1)
                if not first:
                    for q, kind, u in placed(i, 1):
                        unit(b - 1, q, kind, u)

            run(act, step1)

            act.wait_ge(fin_up, 3)
            nc.scalar.activation(FT[:, 0, :], FV, ACT.Sqrt, bias=EPS).then_inc(fin_sg, 1)
            act.wait_ge(scl_up, 1)

            def gate(out, in_, branch):
                return nc.scalar.activation(out, in_, ACT.Sigmoid, scale=SCL[:, 0, branch:branch + 1],
                                            bias=SCL[:, 1, branch:branch + 1])

            act.wait_ge(z1_in, 16)
            gate(Z1F, Z1F, 0).then_inc(g1_up, 1)
            act.wait_ge(sel_up, 1)

            def step2(b, i, first, last):
                g, t = i // T, i % T
                e = b * HALVES + g
                if not last and t == 1:
                    if later(b) or g:
                        act.wait_ge(pool, 9 * e)
                    act.wait_ge(z2_in, (e + 1) * 16)
                    gate(G2F.rearrange("p (k j w) -> p j k w", j=4, w=W),
                         G2Z.rearrange("p (j k w) -> p j k w", j=4, w=W), 1).then_inc(g2_up, 1)
                if not last and t == 2:
                    act.wait_ge(z34_in, (e + 1) * 16)
                    for s in range(2):
                        ins = gate(dims(G34F, s * W, (4 * W, 4), (2 * W, 2), (1, W)),
                                   dims(G34Z, s * N34, (2 * N34, 4), (W, 2), (1, W)), 2 + s)
                    ins.then_inc(g34_up, 1)
                if lagged(i, 9, first, last):
                    j, m = (i - 9) % STEPS, at(b, i - 9)
                    if not (first and i < 11):
                        act.wait_ge(scaled, m - 1)
                    for gr in range(G2):
                        act.wait_ge(gates_mm, m * G2 + gr + 1)
                        nb = min(3, CHUNKS - 3 * gr)
                        bank = (3 * j + gr) % 2 * 3
                        nc.scalar.activation(
                            AB[:, j % 2, 3 * CH * gr:3 * CH * gr + nb * CH].rearrange("p (n c) -> p n c", c=CH),
                            PS[:, bank:bank + nb, 0:CH], ACT.Identity, scale=R4[:, j // T, j % T:j % T + 1],
                            bias=ONES[:, 0:1]).then_inc(a_up, 1)

            run(act, step2)

        @block.vector
        def _(dve):
            count = [0]

            def link(ins):
                count[0] += 1
                ins.then_inc(chain, 1)
                dve.wait_ge(chain, count[0])

            link(nc.vector.memset(P34.rearrange("p a b c -> p (a b c)"), 0.0))
            link(nc.vector.memset(ONES, 1.0))
            link(nc.vector.memset(PICK, 0.0))
            link(nc.vector.memset(PICK[:, CSR - 1:CSR], 1.0))
            link(nc.vector.memset(FIN.rearrange("p a b -> p (a b)"), 0.0))
            nc.vector.memset(EPS, EPS_).then_inc(dve_init, 1)

            dve.wait_ge(consts_in, CONSTS)

            def weights(i, kind0, kind1):
                link(nc.vector.tensor_scalar(WK, WB[:, i, 0:27], KIND[:, kind0:kind0 + 1], None, ALU.mult))
                link(nc.vector.scalar_tensor_tensor(out=WK, in0=WB[:, i, 27:54], scalar=KIND[:, kind1:kind1 + 1],
                                                    in1=WK, op0=ALU.mult, op1=ALU.add))

            for branch in range(3):
                weights(1 + branch, 0, 1 if branch == 0 else 2)
                link(nc.vector.memset(R9.rearrange("p a b c -> p (a b c)"), 0.0))
                for a in range(3):
                    src = dims(WK, 3 * a, (9, 3), (1, 3)) if branch == 0 else dims(WK, 9 * a, (3, 3), (1, 3))
                    link(nc.vector.tensor_copy(R9[:, :, 5 - a, :], src))
                link(nc.vector.tensor_scalar(RP.rearrange("p a b c -> p a (b c)"), dims(R9, 0, (27, 3), (1, 24)),
                                             KIND[:, 3:4], None, ALU.mult))
                link(nc.vector.scalar_tensor_tensor(
                    out=RP.rearrange("p a b c -> p a (b c)"), in0=dims(R9, 3, (27, 3), (1, 24)), scalar=KIND[:, 4:5],
                    in1=RP.rearrange("p a b c -> p a (b c)"), op0=ALU.mult, op1=ALU.add))
                for qo in range(3):
                    band = dims(BAND, (branch * 9 + qo * 3) * MOUT, (MOUT, 3), (4, CT), (1, 4))[0:KIN]
                    tmp = dims(TMP, 0, (MOUT, 3), (4, CT), (1, 4))[0:KIN]
                    for dc in range(3):
                        link(nc.vector.tensor_tensor(tmp if dc else band,
                                                     dims(MASK, dc * CT, (0, 3), (1, CT), (0, 4))[0:KIN],
                                                     dims(RP, dc * 24 + (4 - 2 * qo) * 3, (1, 3), (0, CT), (3, 4))[0:KIN],
                                                     ALU.mult))
                        if dc:
                            link(nc.vector.tensor_tensor(band, band, tmp, ALU.add))
            weights(0, 5, 6)
            band = BAND1[0:2 * H].rearrange("p a b -> p (a b)")
            for dh in range(3):
                link(nc.vector.tensor_tensor(
                    (TMP[0:2 * H] if dh else band).rearrange("p (a b c) -> p a b c", a=3, b=3),
                    dims(MASK1, dh * H, (0, 3), (0, 3), (1, H))[0:2 * H],
                    dims(WK, dh * 3, (9, 3), (1, 3), (0, H))[0:2 * H], ALU.mult))
                if dh:
                    link(nc.vector.tensor_tensor(band, band, TMP[0:2 * H], ALU.add))
            nc.vector.memset(TMP[:, 0:1], 0.0).then_inc(bands_up, 1)

            def stat(e, q, kind, u):
                if kind == "t":
                    return
                dve.wait_ge(unit_out, e * NU + q + 1)
                if kind == "2":
                    ins = nc.vector.bn_stats(S2[0:MOUT, e, u, :], Z2B[0:MOUT, u % RING2, :])
                elif kind == "34":
                    for s in range(2):
                        ins = nc.vector.bn_stats(S34[0:MOUT, s, e, u, :], Z34B[0:MOUT, u % RING34, s * N34:(s + 1) * N34])
                else:
                    ins = nc.vector.bn_stats(S1[0:H, e, u, :], Z1B[0:H, u, :])
                ins.then_inc(unit_stat, 1)

            def step1(b, i, first, last):
                n = at(b, i)
                tile_here = lagged(i, 2, first, last)
                if tile_here:
                    j, m = (i - 2) % STEPS, at(b, i - 2)
                    g, t, slot = j // T, j % T, j % SLOTS
                    v = V[:, slot, :]
                    if t == 0 and not first:
                        dve.wait_ge(p34_out[g], b * 16)
                        dve.wait_ge(p2_out[g], b * 16)

                def over_channels(gr):
                    dve.wait_ge(transposed, m * NGRP + gr + 1)
                    nc.vector.tensor_reduce(over_c(g, t, gr * PER)[0:BLK],
                                            dims(PS[:, :, :], gr % 2 * 1024, (P, PER), (1, P))[0:BLK],
                                            AX.X, ALU.max).then_inc(c_maxed, 1)

                if i == 2 and not first:
                    dve.wait_ge(c_maxed, at(b, 0) * NGRP)
                    nc.vector.tensor_tensor(CB[0:BLK], CM[0:BLK, 0, :], CM[0:BLK, 1, :], ALU.max).then_inc(cb_up, 1)
                    dve.wait_ge(cb_up, b)
                if tile_here:
                    dve.wait_ge(v_up, m + 1)
                    nc.vector.tensor_reduce(pooled(g, 0, t, 1), v.rearrange("p (h w) -> p h w", w=W), AX.X, ALU.max)
                    over_channels(0)
                    nc.vector.tensor_reduce(pooled(g, 0, t, 0), v.rearrange("p (h w) -> p w h", w=W), AX.X, ALU.max)
                    over_channels(1)
                if not last:
                    g0, t0, p0 = i // T, i % T, i % 2
                    dve.wait_ge(mean_mm, n + 1)
                    if t0 == 0 and not first:
                        dve.wait_ge(st_out[g0], b * 16)
                    nc.vector.tensor_copy(RM[:, g0, 0, t0:t0 + 1], PS[:, STAT, 0:1]).then_inc(md_copied, 1)
                    nc.vector.tensor_copy(MD[:, p0, 0:1], PS[:, STAT, 1:2]).then_inc(md_copied, 1)
                    dve.wait_ge(md_copied, 2 * n + 2)
                    dve.wait_ge(squared, n + 1)
                    nc.vector.scalar_tensor_tensor(out=ER[:, p0:p0 + 1], in0=MD[:, p0, 0:1], scalar=MD[:, p0, 0:1],
                                                   in1=SQ[:, p0:p0 + 1], op0=ALU.mult, op1=ALU.add).then_inc(e_up, 1)
                if not first:
                    for q, kind, u in late(i):
                        stat(b - 1, q, kind, u)
                if tile_here:
                    if t == 0:
                        if first:
                            dve.wait_ge(*((pads_out, PADS) if g else (zeros_up, 1)))
                        nc.vector.tensor_copy(plane(g, 0), tile_rows(slot))
                    else:
                        dve.wait_ge(maxed, m)
                        nc.vector.tensor_tensor(plane(g, 0), plane(g, 0), tile_rows(slot), ALU.max)
                    over_channels(2)
                if not first:
                    for q, kind, u in placed(i, 0):
                        stat(b - 1, q, kind, u)
                if not last:
                    dve.wait_ge(sigma, n + 1)
                    nc.vector.reciprocal(RM[:, g0, 1, t0:t0 + 1], SG[:, p0:p0 + 1]).then_inc(r_up, 1)
                    dve.wait_ge(r_up, n + 1)
                    nc.vector.tensor_tensor(NMR[:, p0:p0 + 1], RM[:, g0, 0, t0:t0 + 1], RM[:, g0, 1, t0:t0 + 1],
                                            ALU.mult).then_inc(rm_up, 1)
                if tile_here:
                    nc.vector.tensor_reduce(pooled(g, 1, t, 1), v.rearrange("p (h w) -> p h w", w=W), AX.X,
                                            ALU.add).then_inc(maxed, 1)
                    over_channels(3)
                if not first:
                    for q, kind, u in placed(i, 1):
                        stat(b - 1, q, kind, u)

            run(dve, step1)

            dve.wait_ge(unit_stat, B * len(counted))
            full = 6 * (UNITS2 - 2)
            link(nc.vector.bn_aggr(FIN[0:H, 0, 0:2], S1[0:H].rearrange("p a b c -> p (a b c)")))
            link(nc.vector.bn_aggr(FIN[0:MOUT, 1, 0:2], dims(S2, 0, (6 * UNITS2, B), (1, full))[0:MOUT]))
            link(nc.vector.bn_aggr(FIN[0:MLAST, 1, 2:4], dims(S2, full, (6 * UNITS2, B), (1, 12))[0:MLAST]))
            for s in range(2):
                at_s = s * B * NCT * 6
                link(nc.vector.bn_aggr(FIN[0:MOUT, 2 + s, 0:2], dims(S34, at_s, (6 * NCT, B), (1, 6 * NCT - 6))[0:MOUT]))
                link(nc.vector.bn_aggr(FIN[0:MLAST, 2 + s, 2:4],
                                       dims(S34, at_s + 6 * NCT - 6, (6 * NCT, B), (1, 6))[0:MLAST]))
            nc.vector.memset(TMP[:, 0:1], 0.0).then_inc(fin_up, 1)
            dve.wait_ge(fin_mm, 1)
            weight = KG[:, 0:16].rearrange("p (a b) -> p a b", a=4)
            link(nc.vector.tensor_tensor(FT, PS[:, STAT, 0:16].rearrange("p (a b) -> p a b", a=4), weight, ALU.mult))
            link(nc.vector.tensor_tensor(FM, FT[:, :, 0:2], FT[:, :, 2:4], ALU.add))
            link(nc.vector.tensor_tensor(FD, dims(FIN, 0, (4, 4), (2, 2)), dims(FM, 0, (2, 4), (0, 2)), ALU.subtract))
            link(nc.vector.tensor_tensor(FD, FD, FD, ALU.mult))
            nc.vector.tensor_tensor(FD, FD, KG[:, 16:24].rearrange("p (a b) -> p a b", a=4), ALU.mult).then_inc(fin_up, 1)
            dve.wait_ge(fin_mm, 2)
            link(nc.vector.tensor_tensor(FT[:, :, 0:2], PS[:, STAT, 16:24].rearrange("p (a b) -> p a b", a=4),
                                         dims(KG, 0, (4, 4), (2, 2)), ALU.mult))
            link(nc.vector.tensor_tensor(FV, FT[:, :, 0], FT[:, :, 1], ALU.add))
            nc.vector.tensor_tensor(FV, FV, FM[:, :, 1], ALU.add).then_inc(fin_up, 1)
            dve.wait_ge(fin_sg, 1)
            link(nc.vector.reciprocal(FT[:, 1, :], FT[:, 0, :]))
            link(nc.vector.tensor_tensor(SCL[:, 0, :], GB[:, 0:4], FT[:, 1, :], ALU.mult))
            link(nc.vector.tensor_tensor(FT[:, 2, :], FM[:, :, 0], SCL[:, 0, :], ALU.mult))
            nc.vector.tensor_tensor(SCL[:, 1, :], GB[:, 4:8], FT[:, 2, :], ALU.subtract).then_inc(scl_up, 1)

            dve.wait_ge(sel_in, 16)
            for a in range(2):
                link(nc.vector.tensor_copy(SELR[0:TEAR, a, :], G2F[0:TEAR, :]))
            link(nc.vector.memset(GT[96:P, :, 0, :], 1.0))
            nc.vector.tensor_copy(IDB, IDN).then_inc(sel_up, 1)
            dve.wait_ge(g1_up, 1)
            link(nc.vector.tensor_copy(Z1P[:, 0, :], Z1F))
            link(nc.vector.tensor_tensor(Z1F, Z1F, Z1P[:, 0, :], ALU.subtract))
            link(nc.vector.tensor_copy(Z1P[:, 1, :], Z1F))
            nc.vector.tensor_tensor(Z1P[:, 2, :], Z1F, Z1P[:, 1, :], ALU.subtract).then_inc(g1_split, 1)

            def step2(b, i, first, last):
                if lagged(i, 8, first, last):
                    j, m = (i - 8) % STEPS, at(b, i - 8)
                    dve.wait_ge(gt_mm, m + 1)
                    if not (first and i < 10):
                        dve.wait_ge(gates_mm, (m - 1) * G2)
                    nc.vector.tensor_copy(GT[0:TEAR, j % 2].rearrange("p a b -> p (a b)"),
                                          PS[0:TEAR, 7, 0:3 * P // 2].bitcast(BF16)).then_inc(gt_up, 1)
                if lagged(i, 9, first, last):
                    j, m = (i - 9) % STEPS, at(b, i - 9)
                    e = b if i >= 9 else b - 1
                    g, t, slot = j // T, j % T, j % SLOTS
                    v, mean = V[:, slot, :], RM2[:, g, 0, t:t + 1]
                    dve.wait_ge(y_in[slot], (e * (STEPS // SLOTS) + j // SLOTS + 1) * 16)
                    dve.wait_ge(rm_in, (e * HALVES + g + 1) * 16)
                    dve.wait_ge(a_up, (m + 1) * G2)
                    nc.vector.scalar_tensor_tensor(out=v, in0=v, scalar=mean, in1=AB[:, j % 2, :], op0=ALU.add,
                                                   op1=ALU.mult).then_inc(scaled, 1)
                    dve.wait_ge(scaled, m + 1)
                    nc.vector.tensor_scalar(v, v, mean, None, ALU.subtract).then_inc(done, 1)

            run(dve, step2)

        @block.tensor
        def _(pe):
            def unit(e, q, kind, u):
                pe.wait_ge(unit_out, e * NU + max(q - 1, 0))
                bank = PS[:, CONV + q % 2, :]
                if kind == "t":
                    pe.wait_ge(cb_up, e + 1)
                    for th in range(2):
                        last = nc.tensor.transpose(bank[0:BLK, th * BLK:(th + 1) * BLK],
                                                   CB[0:BLK, th * BLK:(th + 1) * BLK], IDN[0:BLK, 0:BLK])
                    last.then_inc(unit_mm, 1)
                    return
                order = [(a, dw) for dw in (1, 0, 2) for a in range(3)]
                if kind == "2":
                    pe.wait_ge(in2[u % RING2], (e * (UNITS2 // RING2) + u // RING2 + 1) * 16)
                    jobs = [(bank[0:MOUT, 0:N2], BAND[0:KIN, 0], IN2B[0:KIN, u % RING2, :], 2 * W, W, N2 // W)]
                elif kind == "34":
                    pe.wait_ge(in34[u % RING34], (e * (NCT // RING34) + u // RING34 + 1) * 16)
                    jobs = [(bank[0:MOUT, s * N34:(s + 1) * N34], BAND[0:KIN, 1 + s],
                             IN34B[0:KIN, u % RING34, s * PL34:(s + 1) * PL34], 2 * W, W, N34 // W) for s in range(2)]
                else:
                    pe.wait_ge(in1[u], (e + 1) * 48)
                    number = 0
                    for dw in (1, 0, 2):
                        spans = {0: [(CQ, 0, W - CQ), (1, W - CQ, CQ - 1)], 1: [(0, 0, W)],
                                 2: [(0, CQ, W - CQ), (W - CQ, 1, CQ - 1)]}[dw]
                        for a in range(3):
                            for to, from_, width in spans:
                                dst = bank[0:H, 0:T // 2 * W].rearrange("p (r w) -> p r w", w=W)[:, :, to:to + width]
                                last = nc.tensor.matmul(
                                    dst, BAND1[0:2 * H, a * 3 + dw, :],
                                    dims(IN1B[0:2 * H, u, :], a * W + from_, (W, T // 2), (1, width)),
                                    start=(number == 0), stop=(number == 14), skip_group_check=True)
                                number += 1
                    last.then_inc(unit_mm, 1)
                    return
                for out_, band_, in_, stride, shift, rows in jobs:
                    for number, (a, dw) in enumerate(order):
                        lo, hi = max(0, 1 - dw), min(W, W + 1 - dw)
                        src = dims(in_, a * shift + lo + dw - 1, (stride, rows), (1, hi - lo))
                        dst = out_.rearrange("p (r w) -> p r w", w=W)[:, :, lo:hi]
                        last = nc.tensor.matmul(dst, band_[:, a * 3 + dw, :], src, start=(number == 0),
                                                stop=(number == 8), skip_group_check=True)
                last.then_inc(unit_mm, 1)

            pe.wait_ge(consts_in, CONSTS)
            pe.wait_ge(dve_init, 1)

            def step1(b, i, first, last):
                n = at(b, i)
                tile_here = lagged(i, 2, first, last)
                j, m = (i - 2) % STEPS, at(b, i - 2)
                slot = j % SLOTS

                def turn(gr):
                    if not tile_here:
                        return
                    if gr == 0:
                        pe.wait_ge(v_up, m + 1)
                    if not (first and i == 2 and gr < 2):
                        pe.wait_ge(c_maxed, m * NGRP + gr - 1)
                    for k in range(PER * gr, PER * (gr + 1)):
                        at_ = gr % 2 * 1024 + (k - PER * gr) * P
                        ins = nc.tensor.transpose(dims(PS[:, :, :], at_, (1, P))[0:BLK], blocks(slot, k), IDN)
                    ins.then_inc(transposed, 1)
                    if gr == 0 and j == 0 and not first:
                        pe.wait_ge(cs_up, b)
                    for ch in range(CHUNKS)[2 * gr:2 * gr + 2]:
                        row = j % T * CHUNKS + ch
                        ins = nc.tensor.matmul(PS[0:CSR, SUMS, 0:CH], PICK[:, CSR - 1 - row:2 * CSR - 1 - row],
                                               V[:, slot, ch * CH:(ch + 1) * CH], start=(j == 0 and ch == 0),
                                               stop=(j == STEPS - 1 and ch == CHUNKS - 1), skip_group_check=True)
                    if gr == NGRP - 1:
                        ins.then_inc(c_summed, 1)

                def some(k):
                    if not first:
                        for q, kind, u in placed(i, k):
                            if q == 0:
                                pe.wait_ge(bands_up, 1)
                            unit(b - 1, q, kind, u)

                turn(0)
                turn(1)
                some(0)
                if not last:
                    par = i % 2
                    pe.wait_ge(summed, n + 1)
                    if not (first and i == 0):
                        pe.wait_ge(sigma, n)
                    nc.tensor.matmul(PS[:, STAT, 0:1], GRP[:, 0, :], SUM[:, par:par + 1], start=True, stop=True)
                    nc.tensor.matmul(PS[:, STAT, 1:2], GRP[:, 1, :], SUM[:, par:par + 1], start=True,
                                     stop=True).then_inc(mean_mm, 1)
                turn(2)
                if not last:
                    pe.wait_ge(e_up, n + 1)
                    nc.tensor.matmul(PS[:, STAT, 2:3], GRP[:, 2, :], ER[:, par:par + 1], start=True,
                                     stop=True).then_inc(var_mm, 1)
                some(1)
                turn(3)
                some(2)

            run(pe, step1)

            pe.wait_ge(fin_up, 1)
            nc.tensor.matmul(PS[:, STAT, 0:16], ONES, FIN.rearrange("p a b -> p (a b)"), start=True,
                             stop=True).then_inc(fin_mm, 1)
            pe.wait_ge(fin_up, 2)
            nc.tensor.matmul(PS[:, STAT, 16:24], ONES, FD.rearrange("p a b -> p (a b)"), start=True,
                             stop=True).then_inc(fin_mm, 1)
            pe.wait_ge(sel_up, 1)

            def step2(b, i, first, last):
                if lagged(i, 8, first, last):
                    j, m = (i - 8) % STEPS, at(b, i - 8)
                    e = b if i >= 8 else b - 1
                    g, t = j // T, j % T
                    pe.wait_ge(pool, 9 * (e * HALVES + g + 1))
                    if not (first and i == 8):
                        pe.wait_ge(gt_up, m)
                    for s in range(3):
                        at_ = (t % 4 * 2 + t // 4) * TEAR
                        ins = nc.tensor.transpose(PS[0:TEAR, 7, s * P // 2:(s + 1) * P // 2].bitcast(BF16),
                                                  G34P[:, g, s, at_:at_ + TEAR], IDB)
                    ins.then_inc(gt_mm, 1)
                if lagged(i, 9, first, last):
                    j, m = (i - 9) % STEPS, at(b, i - 9)
                    e = b if i >= 9 else b - 1
                    g = j // T
                    pe.wait_ge(gt_up, m + 1)
                    pe.wait_ge(row_in[j % 2], (e * (STEPS // 2) + j // 2 + 1) * 16)
                    for gr in range(G2):
                        if not (first and i == 9 and gr < 2):
                            pe.wait_ge(a_up, m * G2 + gr - 1)
                        for ch in range(3 * gr, min(CHUNKS, 3 * gr + 3)):
                            dst = PS[:, (3 * j + gr) % 2 * 3 + ch - 3 * gr, 0:CH]
                            cols = slice(ch * CH, (ch + 1) * CH)
                            for s in range(3):
                                k = TEAR + 3 if s == 0 else TEAR
                                nc.tensor.matmul(dst, GT[0:k, j % 2, s, :], SELR[0:k, j % 2, cols], start=(s == 0),
                                                 stop=False)
                            for s in range(3):
                                ins = nc.tensor.matmul(dst, IDB, G2P[:, g, s, cols], start=False, stop=(s == 2))
                        ins.then_inc(gates_mm, 1)

            run(pe, step2)


def constants(B):
    f = np.float32
    eye = np.eye(P)
    blockdiag = np.kron(np.eye(P // GROUP), np.ones((GROUP, GROUP))) / GROUP
    sq = np.stack([eye, -blockdiag / HW, (blockdiag - eye) / HW, blockdiag], 1)
    mask = np.zeros((CIN, 4, 3, CT))
    for d in range(3):
        for c in range(CT):
            mask[c + d, :, d, c] = 1
    mask1 = np.zeros((2, H, 3, H))
    for d in range(3):
        for h in range(H):
            if 0 <= h + d - 1 < H:
                mask1[:, h + d - 1, d, h] = 1
    kind = np.zeros((P, 8))
    q = np.arange(P)
    first = q % 4 < 2
    kind[:, 0], kind[:, 1], kind[:, 2] = first, ~first / T, ~first / H
    kind[:, 3], kind[:, 4] = q % 2 == 0, q % 2 == 1
    kind[:, 5], kind[:, 6] = q < H, (q >= H) / (P * HALVES)
    gate = np.zeros((P, 24))
    weight = gate[:, 0:16].reshape(P, 4, 2, 2)
    weight[:, 0, 0] = 1 / H
    weight[:, 1:, 0] = CT * (NCT - 1) / (P * HALVES) / MOUT
    weight[:, 1:, 1] = (MLAST // 4) / (P * HALVES) / MLAST
    gate[:, 0:16] = weight.reshape(P, 16)
    valid = np.zeros((P, 4, 2))
    valid[:, 0, 0] = q < H
    valid[:, 1:, 0] = (q < MOUT)[:, None]
    valid[:, 1:, 1] = (q < MLAST)[:, None]
    gate[:, 16:] = valid.reshape(P, 8)
    sel = np.zeros((2, W, H, W))
    for a in range(W):
        sel[0, a, :, a] = 1
        sel[1, a, a, :] = 1
    return [("k_sq", sq.astype(f)), ("k_mask", mask.reshape(KIN, 3, CT).astype(f)),
            ("k_mask1", mask1.reshape(2 * H, 3, H).astype(f)), ("k_kind", kind.astype(f)), ("k_gate", gate.astype(f)),
            ("k_sel", sel.reshape(TEAR, HW).astype(f))]


def kernel(x, L0_conv_w_str, L0_conv_w_sr, L0_conv_w_trh, L0_conv_w_trw, L0_conv_gamma, L0_conv_beta):
    from concourse import bacc
    from concourse.bass_utils import run_bass_kernel_spmd

    arrays = [("x", x), ("w_str", L0_conv_w_str), ("w_sr", L0_conv_w_sr), ("w_trh", L0_conv_w_trh),
              ("w_trw", L0_conv_w_trw), ("gamma", L0_conv_gamma), ("beta", L0_conv_beta)]
    arrays += constants(x.shape[0] // T)
    nc = bacc.Bacc("TRN2", target_bir_lowering=False, num_devices=1)
    feed, args = {}, []
    for name, a in arrays:
        a = np.ascontiguousarray(a)
        feed[name] = a
        args.append(nc.dram_tensor(name, a.shape, mybir.dt.from_np(a.dtype), kind="ExternalInput").ap())
    out = nc.dram_tensor("out", x.shape, F32, kind="ExternalOutput").ap()
    build(nc, *args, out)
    r = run_bass_kernel_spmd(nc, [feed], core_ids=[0])
    return r.results[0]["out"]
```

```python
from contextlib import ExitStack

import numpy as np

import concourse.bass as bass
from concourse import mybir

F32 = mybir.dt.float32
BF16 = mybir.dt.bfloat16
ALU = mybir.AluOpType
ACT = mybir.ActivationFunctionType
AX = mybir.AxisListType

P = 128
T = 8
HALVES = 2
STEPS = HALVES * T
GROUP = 8
H = W = 56
HW = H * W
EPS_ = 1e-5
SLOTS = 4
ROWS = 4
AROWS, PROWS = 24, 12
FIRST, SECOND = -3, 3

CT = 29
NCT = -(-P * HALVES // CT)
CIN = CT + 2
KIN = CIN * 4
MOUT = CT * 4
MLAST = 4 * (P * HALVES - CT * (NCT - 1))
CPAD = CT * NCT + 2
PL2 = (H // 2 + 1) * W
PL34 = (T // 2 + 1) * W
ROW2 = 4 * PL2
ROW34 = 4 * 2 * PL34
ODD = PL2 + W
N2 = H // 4 // 2 * W
IN2 = (H // 4 + 1) * W
N34 = T // 4 * W
UNITS2 = 2 * NCT
RING2, RING34, RING1 = 3, 3, 2
RING = {"2": RING2, "34": RING34, "1": RING1}
RB, CQ = 28, 4
NHB, NO = H // RB, W // CQ
BLK = RB * CQ
NBLK = NHB * NO
PER = NO // 2
NGRP = NBLK // PER
CH = 8 * W
CHUNKS = HW // CH
COLS = 32
G2 = -(-CHUNKS // 3)
TEAR = H * 2


def dims(base, offset, *pairs):
    return bass.AP(tensor=base.tensor, offset=base.offset + offset, ap=[list(base.ap[0])] + [list(p) for p in pairs])


def units_of_entry():
    u2, u34 = [("2", u) for u in range(UNITS2)], [("34", u) for u in range(NCT)]
    units = []
    while u2 or u34:
        units += u2[:2] + u34[:1]
        u2, u34 = u2[2:], u34[1:]
    half = (P - 1) // CT * 3
    units = units[:half + 3] + [("t", 0)] + units[half + 3:] + [("1", 0), ("1", 1)]
    steps = [FIRST + q * STEPS // len(units) for q in range(len(units))]
    assert all(steps.count(i) <= 2 for i in steps) and steps[half] >= SECOND and CT * (half // 3) + 1 <= P
    assert steps[units.index(("t", 0))] >= SECOND
    return units, steps


def build(nc, x, w_str, w_sr, w_trh, w_trw, gamma, beta, k_sq, k_mask, k_mask1, k_kind, k_gate, k_sel, out):
    B = x.shape[0] // T
    xt = x.rearrange("(b t) (g c) h w -> b g t c (h w)", t=T, c=P)
    ot = out.rearrange("(b t) (g c) h w -> b g t c (h w)", t=T, c=P)
    ZC = B * T * HW // P
    units, unit_step = units_of_entry()
    NU = len(units)
    counted = [q for q in range(NU) if units[q][0] != "t"]

    ctx = ExitStack()
    with ctx:
        def sem(name):
            return ctx.enter_context(nc.semaphore(name))

        p2_d = nc.dram_tensor("p2_d", [B, CPAD, ROW2], F32)
        p34_d = nc.dram_tensor("p34_d", [B, CPAD, ROW34], F32)
        p1_d = nc.dram_tensor("p1_d", [B, NHB, T + 2, HW // NHB], F32)
        s1_d = nc.dram_tensor("s1_d", [B, T + 2, HW], F32)
        z2_d = nc.dram_tensor("z2_d", [B, CT * NCT, HW], F32)
        z34_d = nc.dram_tensor("z34_d", [B, CT * NCT, T * 2 * W], F32)
        z1_d = nc.dram_tensor("z1_d", [B, T, H, W], F32)
        g1_d = nc.dram_tensor("g1_d", [3, B * T * HW], BF16)
        st_d = nc.dram_tensor("st_d", [B, HALVES, P, 2 * T], F32)

        words = 212800 // 4
        S = ctx.enter_context(nc.sbuf_tensor("S", [P, words], F32))

        def taker(at, end):
            place = [at]

            def take(*shape, dt=F32):
                n = int(np.prod(shape))
                n = n if dt == F32 else n // 2
                at = (place[0] + 7) // 8 * 8
                place[0] = at + n
                assert at + n <= end, (at + n, end)
                v = S[:, at:at + n]
                if dt != F32:
                    v = v.bitcast(dt)
                if len(shape) > 1:
                    names = "abcdef"[:len(shape)]
                    v = v.rearrange(f"p ({' '.join(names)}) -> p {' '.join(names)}", **dict(zip(names, shape)))
                return v
            return take, place

        take, used = taker(0, words)
        V = take(SLOTS, HW)
        IDN = take(P)
        GRP = take(3, P)
        ONES = take(P)
        EPS = take(1)
        CONST = take(2)
        GB = take(8)
        KG = take(24)
        S2 = take(B, UNITS2, 6)
        S34 = take(2, B, NCT, 6)
        S1 = take(B, HALVES, 6)
        FIN = take(4, 4)
        FT = take(4, 4)
        FM = take(4, 2)
        FD = take(4, 2)
        FV = take(4)
        SCL = take(2, 4)
        common_end = used[0]
        ACC = take(HALVES, 2, 2 * PL2)
        HT = take(HW // 2)
        WT = take(PROWS, W // 2)
        JUNK = take(HW, dt=BF16)
        JUNK2 = take(AROWS, W, dt=BF16)
        P34 = take(HALVES, 8, PL34)
        IN2B = take(RING2, IN2)
        IN34B = take(RING34, 2 * PL34)
        IN1B = take(2, (T // 2 + 2) * W)
        CM = take(HALVES, T * NBLK)
        CB = take(T * NBLK)
        CS = take(CH)
        PICK = take(2 * COLS - 1)
        Z2B = take(RING2, N2)
        Z34B = take(RING34, 2 * N34)
        Z1B = take(2, T // 2 * W)
        P1T = Z1B.rearrange("p a n -> p (a n)")
        BAND = take(3, 9, MOUT)
        BAND1 = take(9, H)
        RM = take(HALVES, 2, T)
        SUM = take(2)
        CEN = take(2)
        SQ = take(2)
        ER = take(2)
        SG = take(2)
        NMR = take(2)
        MD = take(2, 2)
        take3, _ = taker(IN2B.offset, IN2B.offset + RING2 * IN2)
        MASK = take3(3, CT)
        MASK1 = take3(3, H)
        KIND = take3(8)
        WB = take3(4, 54)
        WK = take3(27)
        R9 = take3(3, 9, 3)
        RP = take3(3, 8, 3)
        TMP = take3(9 * H)
        take2, used2 = taker(common_end, words)
        G2Z = take2(HW)
        G2F = take2(HW)
        GT = take2(2, 3, P, dt=BF16)
        IDB = take2(P, dt=BF16)
        SELR = take2(ROWS, HW, dt=BF16)
        assert used2[0] <= ACC.offset + 4 * 2 * PL2
        AB = take2(2, HW)
        G2P = take2(2, 3, HW, dt=BF16)
        G34Z = take2(T * 2 * W)
        G34F = take2(T * 2 * W)
        G34P = take2(2, 3, T * 2 * W, dt=BF16)
        RM2 = take2(2, 2, T)
        R4 = take2(2, T)
        take4, _ = taker(AB.offset, AB.offset + 2 * HW)
        Z1F = take4(ZC)
        Z1P = take4(3, ZC, dt=BF16)

        PS = ctx.enter_context(nc.psum_tensor("PS", [P, 8, 512], F32))
        SUMS, STAT, CONV = 4, 5, 6

        consts_in = sem("consts_in")
        x_in = [sem(f"x_in{i}") for i in range(SLOTS)]
        zeros_up = sem("zeros_up")
        pads_out = sem("pads_out")
        pool_init = sem("pool_init")
        dve_init = sem("dve_init")
        chain = sem("chain")
        bands_up = sem("bands_up")
        summed = sem("summed")
        centred = sem("centred")
        squared = sem("squared")
        mean_mm = sem("mean_mm")
        md_copied = sem("md_copied")
        e_up = sem("e_up")
        var_mm = sem("var_mm")
        sigma = sem("sigma")
        r_up = sem("r_up")
        rm_up = sem("rm_up")
        v_up = sem("v_up")
        transposed = sem("transposed")
        c_summed = sem("c_summed")
        cs_up = sem("cs_up")
        maxed = sem("maxed")
        w_summed = sem("w_summed")
        t_summed = sem("t_summed")
        h_tree = sem("h_tree")
        w_tree = sem("w_tree")
        c_maxed = sem("c_maxed")
        cb_up = sem("cb_up")
        p2_out = [sem(f"p2_out{g}") for g in range(HALVES)]
        p34_out = [sem(f"p34_out{g}") for g in range(HALVES)]
        st_out = [sem(f"st_out{g}") for g in range(HALVES)]
        in2 = [sem(f"in2_{i}") for i in range(RING2)]
        in34 = [sem(f"in34_{i}") for i in range(RING34)]
        in1 = [sem(f"in1_{i}") for i in range(2)]
        unit_mm = sem("unit_mm")
        unit_out = sem("unit_out")
        unit_stat = sem("unit_stat")
        z2_out = [sem(f"z2_out{i}") for i in range(RING2)]
        z34_out = [sem(f"z34_out{i}") for i in range(RING34)]
        z1_out = [sem(f"z1_out{i}") for i in range(2)]
        p1_out = sem("p1_out")
        s1_out = sem("s1_out")
        fin_up = sem("fin_up")
        fin_mm = sem("fin_mm")
        fin_sg = sem("fin_sg")
        scl_up = sem("scl_up")
        sel_in = sem("sel_in")
        sel_up = sem("sel_up")
        z1_in = sem("z1_in")
        g1_up = sem("g1_up")
        g1_split = sem("g1_split")
        g1_out = sem("g1_out")
        z2_in = sem("z2_in")
        z34_in = sem("z34_in")
        rm_in = sem("rm_in")
        g2_up = sem("g2_up")
        g34_up = sem("g34_up")
        split = sem("split")
        row_in = [sem(f"row_in{i}") for i in range(ROWS)]
        y_in = [sem(f"y_in{i}") for i in range(SLOTS)]
        gt_mm = sem("gt_mm")
        gt_up = sem("gt_up")
        gates_mm = sem("gates_mm")
        a_up = sem("a_up")
        scaled = sem("scaled")
        done = sem("done")
        y_out = [sem(f"y_out{i}") for i in range(SLOTS)]

        CONSTS = 16 * 12
        PADS = 16 * (2 * (1 + B) + 4)

        def at(b, i):
            return b * STEPS + i

        def later(e):
            return not isinstance(e, int) or e > 0

        def lagged(i, lag, first, last):
            return not (first and i < lag) and not (last and i >= lag)

        def run(eng, step):
            for i in range(STEPS):
                step(0, i, True, False)
            with eng.Fori(1, B) as b:
                for i in range(STEPS):
                    step(b, i, False, False)
            for i in range(STEPS):
                step(B, i, False, True)

        def placed(b, i):
            found = [(b - 1 - unit_step[q] // STEPS, q, *units[q]) for q in range(NU) if unit_step[q] % STEPS == i]
            return [u for u in found if not isinstance(u[0], int) or 0 <= u[0] < B]

        def place(b, i, k):
            return placed(b, i)[k:k + 1]

        def late(b, i):
            return place(b, i - 1, 1) if i else place(b - 1, STEPS - 1, 1)

        def q_of(kind, u):
            return units.index((kind, u))

        def frame_slot(t):
            return t % 2, (t + 1) // 2

        def pooled(g, kind, t, branch):
            p, q = frame_slot(t)
            return P34[:, g, (kind * 2 + p) * 2 + branch, q * W:(q + 1) * W]

        def plane(g, kind):
            return dims(ACC, (g * 2 + kind) * 2 * PL2, (ODD, 2), (W, H // 2), (1, W))

        def tile_rows(slot):
            return V[:, slot, :].rearrange("p (q e w) -> p e q w", e=2, w=W)

        def blocks(slot, k):
            return dims(V[:, slot, :], k // NO * RB * W + k % NO, (NO, BLK))

        def over_c(g, t, k):
            return dims(CM, (g * T + t // 4 * 4) * NBLK + (k // NO * 4 + t % 4) * NO + k % NO, (1, PER))

        def split_gates(eng, copy, ops, e, g):
            eng.wait_ge(g2_up, e + 1)
            eng.wait_ge(g34_up, e + 1)
            k = 9 * e
            for full, rest, parts in ((G2F, G2Z, G2P[:, g]), (G34F, G34Z, G34P[:, g])):
                copy(parts[:, 0, :], full).then_inc(split, 1)
                eng.wait_ge(split, k + 1)
                ops.tensor_tensor(rest, full, parts[:, 0, :], ALU.subtract).then_inc(split, 1)
                eng.wait_ge(split, k + 2)
                copy(parts[:, 1, :], rest).then_inc(split, 1)
                eng.wait_ge(split, k + 3)
                ops.tensor_tensor(parts[:, 2, :], rest, parts[:, 1, :], ALU.subtract).then_inc(split, 1)
                k = k + 4
            eng.wait_ge(rm_in, (e + 1) * 16)
            ops.tensor_tensor(R4[:, g, :], RM2[:, g, 1, :], dims(CONST, 1, (0, T)), ALU.mult).then_inc(split, 1)

        block = ctx.enter_context(nc.Block())

        @block.sync
        def _(sp):
            small = [(IDN, k_sq[:, 0, :]), (GRP, k_sq[:, 1:4, :]), (MASK[0:KIN], k_mask),
                     (MASK1[0:2 * H], k_mask1), (KIND, k_kind),
                     (KG, k_gate),
                     (GB[:, 0:4], gamma.rearrange("(o n) -> o n", o=1).broadcast_to([P, 4])),
                     (GB[:, 4:8], beta.rearrange("(o n) -> o n", o=1).broadcast_to([P, 4]))]
            small += [(WB[:, i, :], w.rearrange("o k a b c -> o (k a b c)").broadcast_to([P, 54]))
                      for i, w in enumerate((w_str, w_sr, w_trh, w_trw))]

            def pads():
                zero = ACC[:, 1].rearrange("p k n -> p (k n)")
                sp.wait_ge(zeros_up, 1)
                for d, n in ((p2_d, ROW2), (p34_d, ROW34)):
                    sp.dma_start(d[:, 0, :], zero[0:B, 0:n]).then_inc(pads_out, 16)
                    for b in range(B):
                        sp.dma_start(d[b, P * HALVES + 1:CPAD, :],
                                     zero[0:CPAD - P * HALVES - 1, 0:n]).then_inc(pads_out, 16)
                for tt in (0, T + 1):
                    sp.dma_start(p1_d[:, :, tt, :].rearrange("b h n -> (b h) n"),
                                 zero[0:NHB * B, 0:HW // NHB]).then_inc(pads_out, 16)
                    sp.dma_start(s1_d[:, tt, :], zero[0:B, 0:HW]).then_inc(pads_out, 16)

            def unit_in(e, kind, u):
                if kind == "t":
                    return
                ring = RING[kind]
                if u >= ring:
                    sp.wait_ge(unit_mm, e * NU + q_of(kind, u - ring) + 1)
                if kind == "2":
                    ct, kc = u // 2, u % 2
                    rows = p2_d[e, CT * ct:CT * ct + CIN, :].rearrange("c (k n) -> (c k) n", k=4)
                    sp.dma_start(IN2B[0:KIN, u % RING2, :], rows[:, kc * 2 * N2:kc * 2 * N2 + IN2]).then_inc(in2[u % RING2], 16)
                elif kind == "34":
                    rows = p34_d[e, CT * u:CT * u + CIN, :].rearrange("c (k n) -> (c k) n", k=4)
                    sp.dma_start(IN34B[0:KIN, u % RING34, :], rows).then_inc(in34[u % RING34], 16)
                else:
                    for hb in (1, 0):
                        rows = p1_d[e, hb, T // 2 * u:T // 2 * u + T // 2 + 2, :].rearrange(
                            "t (o h q) -> h (t o) q", o=NO, q=CQ)
                        sp.dma_start(IN1B[RB * hb:RB * (hb + 1), u, :].rearrange("h (n q) -> h n q", q=CQ),
                                     rows).then_inc(in1[u], 16)
                    rows = s1_d[e, T // 2 * u:T // 2 * u + T // 2 + 2, :].rearrange("t (h w) -> h t w", w=W)
                    sp.dma_start(IN1B[H:2 * H, u, :].rearrange("h (t w) -> h t w", w=W), rows).then_inc(in1[u], 16)

            def unit_store(e, q, kind, u):
                sp.wait_ge(unit_out, e * NU + q + 1)
                if kind == "2":
                    ct, kc = u // 2, u % 2
                    rows = z2_d[e, CT * ct:CT * (ct + 1), :].rearrange("c (j n) -> (c j) n", j=4)
                    sp.dma_start(rows[:, kc * N2:(kc + 1) * N2], Z2B[0:MOUT, u % RING2, :]).then_inc(z2_out[u % RING2], 16)
                elif kind == "34":
                    rows = z34_d[e, CT * u:CT * (u + 1), :].rearrange("c (j n) -> (c j) n", j=4)
                    sp.dma_start(rows, Z34B[0:MOUT, u % RING34, :]).then_inc(z34_out[u % RING34], 16)
                elif kind == "1":
                    sp.dma_start(z1_d[e, T // 2 * u:T // 2 * (u + 1)].rearrange("t h w -> h t w"),
                                 Z1B[0:H, u, :].rearrange("h (t w) -> h t w", w=W)).then_inc(z1_out[u], 16)
                else:
                    m = T // 2 * NO
                    for th in range(2):
                        for hb in range(NHB):
                            rows = p1_d[e, hb, 1 + T // 2 * th:1 + T // 2 * (th + 1), :].rearrange(
                                "t (o n) -> (t o) n", o=NO)
                            src = P1T[hb * m:(hb + 1) * m, th * BLK:(th + 1) * BLK]
                            sp.dma_start(rows, src).then_inc(p1_out, 16)

            def units_in(b, i):
                for e, q, kind, u in placed(b, i) if i < STEPS else placed(b + 1, 0):
                    unit_in(e, kind, u)

            def step1(b, i, first, last):
                if i + 1 == FIRST % STEPS and not last:
                    if not first:
                        sp.wait_ge(unit_mm, b * NU - sum(k >= i for k in unit_step))
                    sp.wait_ge(p2_out[0], (b + 1) * 16)
                    sp.wait_ge(p34_out[0], (b + 1) * 16)
                    sp.wait_ge(pads_out, PADS)
                    assert all(units[q][0] == "1" for q in range(NU) if unit_step[q] >= i)
                if last and i == SECOND + 1:
                    sp.wait_ge(h_tree, 7 * B * STEPS)
                    sp.wait_ge(maxed, B * STEPS)
                    sp.wait_ge(w_summed, B * STEPS)
                    sp.wait_ge(t_summed, B * STEPS)
                    sp.wait_ge(c_summed, B * STEPS)
                    sp.dma_start(G2F[0:TEAR, :], k_sel).then_inc(sel_in, 16)
                if last and SECOND + 2 <= i < SECOND + 2 + SLOTS:
                    k = i - SECOND - 2
                    sp.dma_start(V[:, k, :], xt[0, 0, k]).then_inc(y_in[k], 16)
                if last and i == SECOND + 2 + SLOTS:
                    sp.dma_start(G2Z, z2_d[0, 0:P, :]).then_inc(z2_in, 16)
                if i == SECOND and not first:
                    sp.wait_ge(p34_out[1], b * 16)
                if i + 1 == unit_step[q_of("1", 0)] and not first:
                    sp.wait_ge(p1_out, b * 64)
                    sp.wait_ge(s1_out, b * 16 * CHUNKS)
                for k in () if last else (0, 1) if i == 0 else (i + 1,) if i + 1 < STEPS else ():
                    slot, n = k % SLOTS, at(b, k)
                    if not (first and k < SLOTS):
                        sp.wait_ge(h_tree, 7 * (n - SLOTS + 1))
                        sp.wait_ge(maxed, n - SLOTS + 1)
                        sp.wait_ge(w_summed, n - SLOTS + 1)
                        sp.wait_ge(t_summed, n - SLOTS + 1)
                        sp.wait_ge(c_summed, n - SLOTS + 1)
                    sp.dma_start(V[:, slot, :], xt[b, k // T, k % T]).then_inc(x_in[slot], 16)
                if first and i == 0:
                    for dst, src in small:
                        sp.dma_start(dst, src).then_inc(consts_in, 16)
                if first and i == 2:
                    pads()
                if i + 1 != SECOND:
                    units_in(b, i + 1)
                g = {T + 2: 0, 2: 1}.get(i)
                if (g == 0 and not last) or (g == 1 and not first):
                    e = b if g == 0 else b - 1
                    n = at(e, T * (g + 1))
                    sp.wait_ge(h_tree, 7 * n)
                    sp.wait_ge(maxed, n)
                    sp.wait_ge(t_summed, n)
                    sp.wait_ge(w_summed, n)
                    sp.wait_ge(rm_up, n)
                    sp.dma_start(p2_d[e, 1 + P * g:1 + P * (g + 1), :],
                                 ACC[:, g].rearrange("p k n -> p (k n)")).then_inc(p2_out[g], 16)
                    sp.dma_start(p34_d[e, 1 + P * g:1 + P * (g + 1), :],
                                 P34[:, g].rearrange("p k n -> p (k n)")).then_inc(p34_out[g], 16)
                    sp.dma_start(st_d[e, g], RM[:, g].rearrange("p a n -> p (a n)")).then_inc(st_out[g], 16)
                for e, q, kind, u in placed(b, i - 1) if i else placed(b - 1, STEPS - 1):
                    unit_store(e, q, kind, u)
                if i + 1 == SECOND and not first:
                    e = b - 1
                    sp.wait_ge(cs_up, e + 1)
                    for ch in range(CHUNKS):
                        row = ch % 4 * COLS + ch // 4 * T
                        sp.dma_start(s1_d[e, 1:T + 1, ch * CH:(ch + 1) * CH], CS[row:row + T]).then_inc(s1_out, 16)
                    assert all(units[q][0] == "2" for q in range(NU) if unit_step[q] == SECOND)
                    sp.wait_ge(pads_out, PADS)
                    sp.wait_ge(p2_out[1], (e + 1) * 16)
                    units_in(b, SECOND)

            run(sp, step1)

            for s in z2_out:
                sp.wait_ge(s, 16 * B * UNITS2 // RING2)
            for s in z34_out:
                sp.wait_ge(s, 16 * B * NCT // RING34)
            for s in z1_out:
                sp.wait_ge(s, 16 * B)
            for g in range(HALVES):
                sp.wait_ge(st_out[g], 16 * B)
            sp.wait_ge(unit_stat, B * len(counted))
            sp.wait_ge(unit_mm, B * NU)
            sp.wait_ge(c_maxed, B * STEPS * NGRP)
            sp.wait_ge(p1_out, B * 64)
            sp.wait_ge(s1_out, B * 16 * CHUNKS)
            sp.dma_start(Z1F, z1_d.rearrange("b t h w -> (b t h w)").rearrange("(p n) -> p n", p=P)).then_inc(z1_in, 16)
            g1_rows = g1_d.rearrange("s (n c) -> n s c", c=HW)

            def step2(b, i, first, last):
                n, g, t = at(b, i), i // T, i % T
                if not last and t == 0:
                    if later(b) or g:
                        sp.wait_ge(split, 9 * (b * HALVES + g))
                        sp.dma_start(G2Z, z2_d[b, P * g:P * (g + 1), :]).then_inc(z2_in, 16)
                    sp.dma_start(G34Z, z34_d[b, P * g:P * (g + 1), :]).then_inc(z34_in, 16)
                if not last and t == 2:
                    if not first:
                        sp.wait_ge(done, n - 10)
                    sp.dma_start(RM2[:, g].rearrange("p a n -> p (a n)"), st_d[b, g]).then_inc(rm_in, 16)
                if lagged(i, 10, first, last):
                    j = (i - 10) % STEPS
                    e = b if i >= 10 else b - 1
                    sp.wait_ge(done, n - 9)
                    sp.dma_start(ot[e, j // T, j % T], V[:, j % SLOTS, :]).then_inc(y_out[j % SLOTS], 16)
                if first and i == 7:
                    sp.wait_ge(g1_split, 1)
                    for s in range(3):
                        sp.dma_start(g1_d[s].rearrange("(p n) -> p n", p=P), Z1P[:, s, :]).then_inc(g1_out, 16)
                if lagged(i, 7, first, last):
                    j = (i - 7) % STEPS
                    e = b if i >= 7 else b - 1
                    if first and i == 7:
                        sp.wait_ge(g1_out, 48)
                        sp.wait_ge(sel_up, 1)
                    if not (first and i < 7 + ROWS):
                        sp.wait_ge(gates_mm, (n - 7 - ROWS + 1) * G2)
                    sp.dma_start(SELR[TEAR:TEAR + 3, j % ROWS, :], g1_rows[e * T + j % T]).then_inc(row_in[j % ROWS], 16)
                    if not (first and i < 7 + SLOTS):
                        sp.wait_ge(y_out[j % SLOTS], (e * (STEPS // SLOTS) + j // SLOTS) * 16)
                        sp.dma_start(V[:, j % SLOTS, :], xt[e, j // T, j % T]).then_inc(y_in[j % SLOTS], 16)

            run(sp, step2)
            for s in y_out:
                sp.wait_ge(s, 16 * B * STEPS // SLOTS)

        @block.gpsimd
        def _(eng):
            nc.gpsimd.memset(ACC.rearrange("p a b n -> p (a b n)"), 0.0).then_inc(zeros_up, 1)
            nc.gpsimd.memset(CONST[:, 0:1], 0.0).then_inc(pool_init, 1)
            nc.gpsimd.memset(CONST[:, 1:2], 0.25).then_inc(pool_init, 1)
            eng.wait_ge(pool_init, 2)

            def step1(b, i, first, last):
                if not lagged(i, 2, first, last):
                    return
                j, n = (i - 2) % STEPS, at(b, i - 2)
                g, t = j // T, j % T
                v = V[:, j % SLOTS, :]
                k = 7 * n
                rows = v[:, AROWS * W:(AROWS + PROWS) * W].rearrange("p (h w) -> p h w", w=W)
                eng.wait_ge(v_up, n + 1)
                if not (first and i == 2):
                    eng.wait_ge(h_tree, k)
                nc.gpsimd.tensor_tensor(HT, v[:, 0:HW // 2], v[:, HW // 2:HW], ALU.add).then_inc(h_tree, 1)
                nc.gpsimd.tensor_tensor(WT, rows[:, :, 0:W // 2], rows[:, :, W // 2:W], ALU.add).then_inc(w_tree, 1)
                if t == 0:
                    if not first:
                        eng.wait_ge(p2_out[g], b * 16)
                        eng.wait_ge(p34_out[g], b * 16)
                    elif g:
                        eng.wait_ge(pads_out, PADS)
                    else:
                        eng.wait_ge(zeros_up, 1)
                    nc.gpsimd.tensor_tensor(plane(g, 1), tile_rows(j % SLOTS),
                                            dims(CONST, 0, (0, 2), (0, H // 2), (0, W)), ALU.add).then_inc(t_summed, 1)
                else:
                    eng.wait_ge(t_summed, n)
                    nc.gpsimd.tensor_tensor(plane(g, 1), plane(g, 1), tile_rows(j % SLOTS),
                                            ALU.add).then_inc(t_summed, 1)
                for left in (14, 7, 3):
                    k = k + 1
                    eng.wait_ge(h_tree, k)
                    nc.gpsimd.tensor_tensor(HT[:, 0:left * W], HT[:, 0:left * W], HT[:, left * W:2 * left * W],
                                            ALU.add).then_inc(h_tree, 1)
                    eng.wait_ge(w_tree, k)
                    nc.gpsimd.tensor_tensor(WT[:, :, 0:left], WT[:, :, 0:left], WT[:, :, left:2 * left],
                                            ALU.add).then_inc(w_tree, 1)
                k = k + 1
                eng.wait_ge(h_tree, k)
                nc.gpsimd.tensor_tensor(HT[:, 0:W], HT[:, 0:W], HT[:, 6 * W:7 * W], ALU.add).then_inc(h_tree, 1)
                nc.gpsimd.tensor_tensor(HT[:, W:2 * W], HT[:, W:2 * W], HT[:, 2 * W:3 * W], ALU.add).then_inc(h_tree, 1)
                eng.wait_ge(w_tree, k)
                nc.gpsimd.tensor_tensor(WT[:, :, 0], WT[:, :, 0], WT[:, :, 6], ALU.add).then_inc(w_tree, 1)
                nc.gpsimd.tensor_tensor(WT[:, :, 1], WT[:, :, 1], WT[:, :, 2], ALU.add).then_inc(w_tree, 1)
                eng.wait_ge(w_tree, k + 2)
                nc.gpsimd.tensor_tensor(pooled(g, 1, t, 1)[:, AROWS:AROWS + PROWS], WT[:, :, 0], WT[:, :, 1],
                                        ALU.add).then_inc(w_tree, 1)
                eng.wait_ge(h_tree, k + 2)
                nc.gpsimd.tensor_tensor(pooled(g, 1, t, 0), HT[:, 0:W], HT[:, W:2 * W], ALU.add).then_inc(h_tree, 1)

            run(eng, step1)

            def step2(b, i, first, last):
                def add_zero(dst, src):
                    return nc.gpsimd.tensor_tensor(dst, src, dims(CONST, 0, (0, src.shape[-1])), ALU.add)

                g, t = i // T, i % T
                if last or t != 4 or (first and not g):
                    return
                e, n = b * HALVES + g, at(b, i)
                if not first:
                    eng.wait_ge(gates_mm, (n - 12) * G2)
                    eng.wait_ge(a_up, (n - 12) * G2)
                split_gates(eng, add_zero, nc.gpsimd, e, g)

            run(eng, step2)

        @block.scalar
        def _(act):
            def unit(e, q, kind, u):
                act.wait_ge(unit_mm, e * NU + q + 1)
                src = PS[:, CONV + q % 2, :]
                if kind == "t":
                    for s in z1_out:
                        act.wait_ge(s, e * 16)
                    act.wait_ge(unit_stat, e * len(counted))
                    nc.scalar.copy(P1T[0:BLK, 0:2 * BLK], src[0:BLK, 0:2 * BLK]).then_inc(unit_out, 1)
                    return
                ring = RING[kind]
                outs = {"2": z2_out, "34": z34_out, "1": z1_out}[kind]
                per = {"2": UNITS2, "34": NCT, "1": 2}[kind] // ring
                act.wait_ge(outs[u % ring], (e * per + u // ring) * 16)
                before = counted.index(q_of(kind, u - ring)) + 1 if u >= ring else 0
                act.wait_ge(unit_stat, e * len(counted) + before)
                dst, m, width = {"2": (Z2B, MOUT, N2), "34": (Z34B, MOUT, 2 * N34), "1": (Z1B, H, T // 2 * W)}[kind]
                dst, src = dst[0:m, u % ring, :], src[0:m, 0:width]
                if kind == "1":
                    dst = dst.rearrange("p (t q o) -> p t o q", q=CQ, o=NO)
                    src = src.rearrange("p (t o q) -> p t o q", q=CQ, o=NO)
                nc.scalar.copy(dst, src).then_inc(unit_out, 1)

            act.wait_ge(dve_init, 1)

            def step1(b, i, first, last):
                n = at(b, i)
                if i == 2 and not first:
                    act.wait_ge(c_summed, at(b, 0))
                    if later(b - 1):
                        act.wait_ge(s1_out, (b - 1) * 16 * CHUNKS)
                    nc.scalar.copy(CS.rearrange("p (h o q) -> p h q o", o=NO, q=CQ),
                                   PS[:, SUMS, 0:CH].rearrange("p (h q o) -> p h q o", o=NO, q=CQ)).then_inc(cs_up, 1)
                if not last:
                    slot, par = i % SLOTS, i % 2
                    act.wait_ge(x_in[slot], (b * (STEPS // SLOTS) + i // SLOTS + 1) * 16)
                    if not (first and i == 0):
                        act.wait_ge(squared, n)
                    nc.scalar.activation(JUNK, V[:, slot, :], ACT.Copy,
                                         accum_out=SUM[:, par:par + 1]).then_inc(summed, 1)
                    act.wait_ge(summed, n + 1)
                    nc.scalar.mul(CEN[:, par:par + 1], SUM[:, par:par + 1], -1.0 / (HW * W)).then_inc(centred, 1)
                if lagged(i, 1, first, last):
                    j = (i - 1) % STEPS
                    act.wait_ge(rm_up, n)
                    v = V[:, j % SLOTS, :]
                    nc.scalar.activation(v, v, ACT.Identity, scale=RM[:, j // T, 1, j % T:j % T + 1],
                                         bias=NMR[:, j % 2:j % 2 + 1]).then_inc(v_up, 1)
                for e, q, kind, u in late(b, i):
                    unit(e, q, kind, u)
                if not last:
                    act.wait_ge(centred, n + 1)
                    nc.scalar.activation(JUNK, V[:, slot, :], ACT.Square, scale=1.0 / W, bias=CEN[:, par:par + 1],
                                         accum_out=SQ[:, par:par + 1]).then_inc(squared, 1)
                if lagged(i, 2, first, last):
                    j, m = (i - 2) % STEPS, at(b, i - 2)
                    g, t = j // T, j % T
                    act.wait_ge(v_up, m + 1)
                    if not (first and i == 2):
                        act.wait_ge(w_summed, m)
                    if t == 0 and not first:
                        act.wait_ge(p34_out[g], b * 16)
                    sums = pooled(g, 1, t, 1)
                    for h in range(AROWS):
                        ins = nc.scalar.activation(JUNK2[:, h, :], V[:, j % SLOTS, h * W:(h + 1) * W], ACT.Copy,
                                                   accum_out=sums[:, h:h + 1])
                    ins.then_inc(w_summed, 1)
                for e, q, kind, u in place(b, i, 0):
                    unit(e, q, kind, u)
                if not last:
                    act.wait_ge(var_mm, n + 1)
                    nc.scalar.activation(SG[:, par:par + 1], PS[:, STAT, 2:3], ACT.Sqrt, bias=EPS).then_inc(sigma, 1)

            run(act, step1)

            act.wait_ge(fin_up, 3)
            nc.scalar.activation(FT[:, 0, :], FV, ACT.Sqrt, bias=EPS).then_inc(fin_sg, 1)
            act.wait_ge(scl_up, 1)

            def gate(out, in_, branch):
                return nc.scalar.activation(out, in_, ACT.Sigmoid, scale=SCL[:, 0, branch:branch + 1],
                                            bias=SCL[:, 1, branch:branch + 1])

            act.wait_ge(z1_in, 16)
            gate(Z1F, Z1F, 0).then_inc(g1_up, 1)
            act.wait_ge(sel_up, 1)

            def step2(b, i, first, last):
                g, t = i // T, i % T
                e = b * HALVES + g
                if lagged(i, 9, first, last):
                    j, m = (i - 9) % STEPS, at(b, i - 9)
                    if not (first and i < 11):
                        act.wait_ge(scaled, m - 1)
                    for gr in range(G2):
                        act.wait_ge(gates_mm, m * G2 + gr + 1)
                        nb = min(3, CHUNKS - 3 * gr)
                        bank = (3 * j + gr) % 2 * 3
                        nc.scalar.activation(
                            AB[:, j % 2, 3 * CH * gr:3 * CH * gr + nb * CH].rearrange("p (n c) -> p n c", c=CH),
                            PS[:, bank:bank + nb, 0:CH], ACT.Identity, scale=R4[:, j // T, j % T:j % T + 1],
                            bias=ONES[:, 0:1]).then_inc(a_up, 1)
                if not last and t == 2:
                    if later(b) or g:
                        act.wait_ge(split, 9 * e)
                    act.wait_ge(z2_in, (e + 1) * 16)
                    gate(G2F.rearrange("p (k j w) -> p j k w", j=4, w=W),
                         G2Z.rearrange("p (j k w) -> p j k w", j=4, w=W), 1).then_inc(g2_up, 1)
                    act.wait_ge(z34_in, (e + 1) * 16)
                    for s in range(2):
                        ins = gate(dims(G34F, s * W, (4 * W, 4), (2 * W, 2), (1, W)),
                                   dims(G34Z, s * N34, (2 * N34, 4), (W, 2), (1, W)), 2 + s)
                    ins.then_inc(g34_up, 1)

            run(act, step2)

        @block.vector
        def _(dve):
            count = [0]

            def link(ins):
                count[0] += 1
                ins.then_inc(chain, 1)
                dve.wait_ge(chain, count[0])

            link(nc.vector.memset(P34.rearrange("p a b c -> p (a b c)"), 0.0))
            link(nc.vector.memset(ONES, 1.0))
            link(nc.vector.memset(PICK, 0.0))
            link(nc.vector.memset(PICK[:, COLS - 1:COLS], 1.0))
            link(nc.vector.memset(FIN.rearrange("p a b -> p (a b)"), 0.0))
            nc.vector.memset(EPS, EPS_).then_inc(dve_init, 1)

            dve.wait_ge(consts_in, CONSTS)

            def weights(i, kind0, kind1):
                link(nc.vector.tensor_scalar(WK, WB[:, i, 0:27], KIND[:, kind0:kind0 + 1], None, ALU.mult))
                link(nc.vector.scalar_tensor_tensor(out=WK, in0=WB[:, i, 27:54], scalar=KIND[:, kind1:kind1 + 1],
                                                    in1=WK, op0=ALU.mult, op1=ALU.add))

            def bands(branch):
                weights(1 + branch, 0, 1 if branch == 0 else 2)
                link(nc.vector.memset(R9.rearrange("p a b c -> p (a b c)"), 0.0))
                for a in range(3):
                    src = dims(WK, 3 * a, (9, 3), (1, 3)) if branch == 0 else dims(WK, 9 * a, (3, 3), (1, 3))
                    link(nc.vector.tensor_copy(R9[:, :, 5 - a, :], src))
                link(nc.vector.tensor_scalar(RP.rearrange("p a b c -> p a (b c)"), dims(R9, 0, (27, 3), (1, 24)),
                                             KIND[:, 3:4], None, ALU.mult))
                link(nc.vector.scalar_tensor_tensor(
                    out=RP.rearrange("p a b c -> p a (b c)"), in0=dims(R9, 3, (27, 3), (1, 24)), scalar=KIND[:, 4:5],
                    in1=RP.rearrange("p a b c -> p a (b c)"), op0=ALU.mult, op1=ALU.add))
                for qo in range(3):
                    band = dims(BAND, (branch * 9 + qo * 3) * MOUT, (MOUT, 3), (4, CT), (1, 4))[0:KIN]
                    tmp = dims(TMP, 0, (MOUT, 3), (4, CT), (1, 4))[0:KIN]
                    for dc in range(3):
                        link(nc.vector.tensor_tensor(tmp if dc else band,
                                                     dims(MASK, dc * CT, (0, 3), (1, CT), (0, 4))[0:KIN],
                                                     dims(RP, dc * 24 + (4 - 2 * qo) * 3, (1, 3), (0, CT), (3, 4))[0:KIN],
                                                     ALU.mult))
                        if dc:
                            link(nc.vector.tensor_tensor(band, band, tmp, ALU.add))

            def bands1():
                weights(0, 5, 6)
                band = BAND1[0:2 * H].rearrange("p a b -> p (a b)")
                for dh in range(3):
                    link(nc.vector.tensor_tensor(
                        (TMP[0:2 * H] if dh else band).rearrange("p (a b c) -> p a b c", a=3, b=3),
                        dims(MASK1, dh * H, (0, 3), (0, 3), (1, H))[0:2 * H],
                        dims(WK, dh * 3, (9, 3), (1, 3), (0, H))[0:2 * H], ALU.mult))
                    if dh:
                        link(nc.vector.tensor_tensor(band, band, TMP[0:2 * H], ALU.add))
                nc.vector.memset(TMP[:, 0:1], 0.0).then_inc(bands_up, 1)

            def stat(e, q, kind, u):
                if kind == "t":
                    return
                dve.wait_ge(unit_out, e * NU + q + 1)
                if kind == "2":
                    ins = nc.vector.bn_stats(S2[0:MOUT, e, u, :], Z2B[0:MOUT, u % RING2, :])
                elif kind == "34":
                    for s in range(2):
                        ins = nc.vector.bn_stats(S34[0:MOUT, s, e, u, :], Z34B[0:MOUT, u % RING34, s * N34:(s + 1) * N34])
                else:
                    ins = nc.vector.bn_stats(S1[0:H, e, u, :], Z1B[0:H, u, :])
                ins.then_inc(unit_stat, 1)

            def step1(b, i, first, last):
                n = at(b, i)
                if first and 1 <= i <= 4:
                    bands(i - 1) if i < 4 else bands1()
                if last and i == SECOND + 2:
                    dve.wait_ge(sel_in, 16)
                    for a in range(ROWS):
                        link(nc.vector.tensor_copy(SELR[0:TEAR, a, :], G2F[0:TEAR, :]))
                    link(nc.vector.memset(GT[96:P, :, 0, :], 1.0))
                    nc.vector.tensor_copy(IDB, IDN).then_inc(sel_up, 1)
                tile_here = lagged(i, 2, first, last)
                if tile_here:
                    j, m = (i - 2) % STEPS, at(b, i - 2)
                    g, t, slot = j // T, j % T, j % SLOTS
                    v = V[:, slot, :]
                    if t == 0 and not first:
                        dve.wait_ge(p34_out[g], b * 16)
                        dve.wait_ge(p2_out[g], b * 16)

                def over_channels(gr):
                    dve.wait_ge(transposed, m * NGRP + gr + 1)
                    nc.vector.tensor_reduce(over_c(g, t, gr * PER)[0:BLK],
                                            dims(PS[:, :, :], gr % 2 * 1024, (P, PER), (1, P))[0:BLK],
                                            AX.X, ALU.max).then_inc(c_maxed, 1)

                if i == 2 and not first:
                    dve.wait_ge(c_maxed, at(b, 0) * NGRP)
                    nc.vector.tensor_tensor(CB[0:BLK], CM[0:BLK, 0, :], CM[0:BLK, 1, :], ALU.max).then_inc(cb_up, 1)
                    dve.wait_ge(cb_up, b)
                if tile_here:
                    dve.wait_ge(v_up, m + 1)
                    nc.vector.tensor_reduce(pooled(g, 0, t, 1), v.rearrange("p (h w) -> p h w", w=W), AX.X, ALU.max)
                    over_channels(0)
                    nc.vector.tensor_reduce(pooled(g, 0, t, 0), v.rearrange("p (h w) -> p w h", w=W), AX.X, ALU.max)
                    over_channels(1)
                if not last:
                    g0, t0, p0 = i // T, i % T, i % 2
                    dve.wait_ge(mean_mm, n + 1)
                    if t0 == 0 and not first:
                        dve.wait_ge(st_out[g0], b * 16)
                    nc.vector.tensor_copy(RM[:, g0, 0, t0:t0 + 1], PS[:, STAT, 0:1]).then_inc(md_copied, 1)
                    nc.vector.tensor_copy(MD[:, p0, 0:1], PS[:, STAT, 1:2]).then_inc(md_copied, 1)
                    dve.wait_ge(md_copied, 2 * n + 2)
                    dve.wait_ge(squared, n + 1)
                    nc.vector.scalar_tensor_tensor(out=ER[:, p0:p0 + 1], in0=MD[:, p0, 0:1], scalar=MD[:, p0, 0:1],
                                                   in1=SQ[:, p0:p0 + 1], op0=ALU.mult, op1=ALU.add).then_inc(e_up, 1)
                if tile_here:
                    if t == 0:
                        if first:
                            dve.wait_ge(*((pads_out, PADS) if g else (zeros_up, 1)))
                        nc.vector.tensor_copy(plane(g, 0), tile_rows(slot))
                    else:
                        dve.wait_ge(maxed, m)
                        nc.vector.tensor_tensor(plane(g, 0), plane(g, 0), tile_rows(slot), ALU.max)
                    over_channels(2)
                for e, q, kind, u in late(b, i) + place(b, i, 0):
                    stat(e, q, kind, u)
                if not last:
                    dve.wait_ge(sigma, n + 1)
                    nc.vector.reciprocal(RM[:, g0, 1, t0:t0 + 1], SG[:, p0:p0 + 1]).then_inc(r_up, 1)
                    dve.wait_ge(r_up, n + 1)
                    nc.vector.tensor_tensor(NMR[:, p0:p0 + 1], RM[:, g0, 0, t0:t0 + 1], RM[:, g0, 1, t0:t0 + 1],
                                            ALU.mult).then_inc(rm_up, 1)
                if tile_here:
                    nc.vector.tensor_reduce(pooled(g, 1, t, 1)[:, AROWS + PROWS:H],
                                            v[:, (AROWS + PROWS) * W:HW].rearrange("p (h w) -> p h w", w=W), AX.X, ALU.add).then_inc(maxed, 1)
                    over_channels(3)

            run(dve, step1)

            dve.wait_ge(unit_stat, B * len(counted))
            full = 6 * (UNITS2 - 2)
            link(nc.vector.bn_aggr(FIN[0:H, 0, 0:2], S1[0:H].rearrange("p a b c -> p (a b c)")))
            link(nc.vector.bn_aggr(FIN[0:MOUT, 1, 0:2], dims(S2, 0, (6 * UNITS2, B), (1, full))[0:MOUT]))
            link(nc.vector.bn_aggr(FIN[0:MLAST, 1, 2:4], dims(S2, full, (6 * UNITS2, B), (1, 12))[0:MLAST]))
            for s in range(2):
                at_s = s * B * NCT * 6
                link(nc.vector.bn_aggr(FIN[0:MOUT, 2 + s, 0:2], dims(S34, at_s, (6 * NCT, B), (1, 6 * NCT - 6))[0:MOUT]))
                link(nc.vector.bn_aggr(FIN[0:MLAST, 2 + s, 2:4],
                                       dims(S34, at_s + 6 * NCT - 6, (6 * NCT, B), (1, 6))[0:MLAST]))
            nc.vector.memset(TMP[:, 0:1], 0.0).then_inc(fin_up, 1)
            dve.wait_ge(fin_mm, 1)
            weight = KG[:, 0:16].rearrange("p (a b) -> p a b", a=4)
            link(nc.vector.tensor_tensor(FT, PS[:, STAT, 0:16].rearrange("p (a b) -> p a b", a=4), weight, ALU.mult))
            link(nc.vector.tensor_tensor(FM, FT[:, :, 0:2], FT[:, :, 2:4], ALU.add))
            link(nc.vector.tensor_tensor(FD, dims(FIN, 0, (4, 4), (2, 2)), dims(FM, 0, (2, 4), (0, 2)), ALU.subtract))
            link(nc.vector.tensor_tensor(FD, FD, FD, ALU.mult))
            nc.vector.tensor_tensor(FD, FD, KG[:, 16:24].rearrange("p (a b) -> p a b", a=4), ALU.mult).then_inc(fin_up, 1)
            dve.wait_ge(fin_mm, 2)
            link(nc.vector.tensor_tensor(FT[:, :, 0:2], PS[:, STAT, 16:24].rearrange("p (a b) -> p a b", a=4),
                                         dims(KG, 0, (4, 4), (2, 2)), ALU.mult))
            link(nc.vector.tensor_tensor(FV, FT[:, :, 0], FT[:, :, 1], ALU.add))
            nc.vector.tensor_tensor(FV, FV, FM[:, :, 1], ALU.add).then_inc(fin_up, 1)
            dve.wait_ge(fin_sg, 1)
            link(nc.vector.reciprocal(FT[:, 1, :], FT[:, 0, :]))
            link(nc.vector.tensor_tensor(SCL[:, 0, :], GB[:, 0:4], FT[:, 1, :], ALU.mult))
            link(nc.vector.tensor_tensor(FT[:, 2, :], FM[:, :, 0], SCL[:, 0, :], ALU.mult))
            nc.vector.tensor_tensor(SCL[:, 1, :], GB[:, 4:8], FT[:, 2, :], ALU.subtract).then_inc(scl_up, 1)

            dve.wait_ge(g1_up, 1)
            link(nc.vector.tensor_copy(Z1P[:, 0, :], Z1F))
            link(nc.vector.tensor_tensor(Z1F, Z1F, Z1P[:, 0, :], ALU.subtract))
            link(nc.vector.tensor_copy(Z1P[:, 1, :], Z1F))
            nc.vector.tensor_tensor(Z1P[:, 2, :], Z1F, Z1P[:, 1, :], ALU.subtract).then_inc(g1_split, 1)

            dve.wait_ge(pool_init, 2)
            split_gates(dve, nc.vector.tensor_copy, nc.vector, 0, 0)

            def step2(b, i, first, last):
                if lagged(i, 8, first, last):
                    j, m = (i - 8) % STEPS, at(b, i - 8)
                    dve.wait_ge(gt_mm, m + 1)
                    if not (first and i < 10):
                        dve.wait_ge(gates_mm, (m - 1) * G2)
                    nc.vector.tensor_copy(GT[0:TEAR, j % 2].rearrange("p a b -> p (a b)"),
                                          PS[0:TEAR, 7, 0:3 * P // 2].bitcast(BF16)).then_inc(gt_up, 1)
                if lagged(i, 9, first, last):
                    j, m = (i - 9) % STEPS, at(b, i - 9)
                    e = b if i >= 9 else b - 1
                    g, t, slot = j // T, j % T, j % SLOTS
                    v, mean = V[:, slot, :], RM2[:, g, 0, t:t + 1]
                    dve.wait_ge(y_in[slot], (e * (STEPS // SLOTS) + j // SLOTS + 1) * 16)
                    dve.wait_ge(rm_in, (e * HALVES + g + 1) * 16)
                    dve.wait_ge(a_up, (m + 1) * G2)
                    nc.vector.scalar_tensor_tensor(out=v, in0=v, scalar=mean, in1=AB[:, j % 2, :], op0=ALU.add,
                                                   op1=ALU.mult).then_inc(scaled, 1)
                    dve.wait_ge(scaled, m + 1)
                    nc.vector.tensor_scalar(v, v, mean, None, ALU.subtract).then_inc(done, 1)

            run(dve, step2)

        @block.tensor
        def _(pe):
            def unit(e, q, kind, u):
                pe.wait_ge(unit_out, e * NU + max(q - 1, 0))
                bank = PS[:, CONV + q % 2, :]
                if kind == "t":
                    pe.wait_ge(cb_up, e + 1)
                    for th in range(2):
                        last = nc.tensor.transpose(bank[0:BLK, th * BLK:(th + 1) * BLK],
                                                   CB[0:BLK, th * BLK:(th + 1) * BLK], IDN[0:BLK, 0:BLK])
                    last.then_inc(unit_mm, 1)
                    return
                order = [(a, dw) for dw in (1, 0, 2) for a in range(3)]
                if kind == "2":
                    pe.wait_ge(in2[u % RING2], (e * (UNITS2 // RING2) + u // RING2 + 1) * 16)
                    jobs = [(bank[0:MOUT, 0:N2], BAND[0:KIN, 0], IN2B[0:KIN, u % RING2, :], 2 * W, W, N2 // W)]
                elif kind == "34":
                    pe.wait_ge(in34[u % RING34], (e * (NCT // RING34) + u // RING34 + 1) * 16)
                    jobs = [(bank[0:MOUT, s * N34:(s + 1) * N34], BAND[0:KIN, 1 + s],
                             IN34B[0:KIN, u % RING34, s * PL34:(s + 1) * PL34], 2 * W, W, N34 // W) for s in range(2)]
                else:
                    pe.wait_ge(in1[u], (e + 1) * 48)
                    number = 0
                    for dw in (1, 0, 2):
                        spans = {0: [(CQ, 0, W - CQ), (1, W - CQ, CQ - 1)], 1: [(0, 0, W)],
                                 2: [(0, CQ, W - CQ), (W - CQ, 1, CQ - 1)]}[dw]
                        for a in range(3):
                            for to, from_, width in spans:
                                dst = bank[0:H, 0:T // 2 * W].rearrange("p (r w) -> p r w", w=W)[:, :, to:to + width]
                                last = nc.tensor.matmul(
                                    dst, BAND1[0:2 * H, a * 3 + dw, :],
                                    dims(IN1B[0:2 * H, u, :], a * W + from_, (W, T // 2), (1, width)),
                                    start=(number == 0), stop=(number == 14), skip_group_check=True)
                                number += 1
                    last.then_inc(unit_mm, 1)
                    return
                for out_, band_, in_, stride, shift, rows in jobs:
                    for number, (a, dw) in enumerate(order):
                        lo, hi = max(0, 1 - dw), min(W, W + 1 - dw)
                        src = dims(in_, a * shift + lo + dw - 1, (stride, rows), (1, hi - lo))
                        dst = out_.rearrange("p (r w) -> p r w", w=W)[:, :, lo:hi]
                        last = nc.tensor.matmul(dst, band_[:, a * 3 + dw, :], src, start=(number == 0),
                                                stop=(number == 8), skip_group_check=True)
                last.then_inc(unit_mm, 1)

            pe.wait_ge(consts_in, CONSTS)
            pe.wait_ge(dve_init, 1)

            def step1(b, i, first, last):
                n = at(b, i)
                tile_here = lagged(i, 2, first, last)
                j, m = (i - 2) % STEPS, at(b, i - 2)
                slot = j % SLOTS

                def turn(gr):
                    if not tile_here:
                        return
                    if gr == 0:
                        pe.wait_ge(v_up, m + 1)
                    if not (first and i == 2 and gr < 2):
                        pe.wait_ge(c_maxed, m * NGRP + gr - 1)
                    for k in range(PER * gr, PER * (gr + 1)):
                        at_ = gr % 2 * 1024 + (k - PER * gr) * P
                        ins = nc.tensor.transpose(dims(PS[:, :, :], at_, (1, P))[0:BLK], blocks(slot, k), IDN)
                    ins.then_inc(transposed, 1)
                    if gr == 1 and j == 0 and not first:
                        pe.wait_ge(cs_up, b)
                    for ch in {1: range(4), 3: range(4, CHUNKS)}.get(gr, ()):
                        row, tile = ch // 4 * T + j % T, ch % 4
                        ins = nc.tensor.matmul(PS[tile * COLS:(tile + 1) * COLS, SUMS, 0:CH],
                                               PICK[:, COLS - 1 - row:2 * COLS - 1 - row],
                                               V[:, slot, ch * CH:(ch + 1) * CH], start=(j == 0 and ch < 4),
                                               stop=(j == STEPS - 1 and ch + 4 >= CHUNKS), skip_group_check=True,
                                               tile_position=(0, tile * COLS))
                    if gr == NGRP - 1:
                        ins.then_inc(c_summed, 1)

                def some(k):
                    for e, q, kind, u in place(b, i, k):
                        if q == 0:
                            pe.wait_ge(bands_up, 1)
                        unit(e, q, kind, u)

                turn(0)
                turn(1)
                if not last:
                    par = i % 2
                    pe.wait_ge(summed, n + 1)
                    if not (first and i == 0):
                        pe.wait_ge(sigma, n)
                    nc.tensor.matmul(PS[:, STAT, 0:1], GRP[:, 0, :], SUM[:, par:par + 1], start=True, stop=True)
                    nc.tensor.matmul(PS[:, STAT, 1:2], GRP[:, 1, :], SUM[:, par:par + 1], start=True,
                                     stop=True).then_inc(mean_mm, 1)
                some(0)
                turn(2)
                if not last:
                    pe.wait_ge(e_up, n + 1)
                    nc.tensor.matmul(PS[:, STAT, 2:3], GRP[:, 2, :], ER[:, par:par + 1], start=True,
                                     stop=True).then_inc(var_mm, 1)
                turn(3)
                some(1)

            run(pe, step1)

            pe.wait_ge(fin_up, 1)
            nc.tensor.matmul(PS[:, STAT, 0:16], ONES, FIN.rearrange("p a b -> p (a b)"), start=True,
                             stop=True).then_inc(fin_mm, 1)
            pe.wait_ge(fin_up, 2)
            nc.tensor.matmul(PS[:, STAT, 16:24], ONES, FD.rearrange("p a b -> p (a b)"), start=True,
                             stop=True).then_inc(fin_mm, 1)
            pe.wait_ge(sel_up, 1)

            def step2(b, i, first, last):
                if lagged(i, 8, first, last):
                    j, m = (i - 8) % STEPS, at(b, i - 8)
                    e = b if i >= 8 else b - 1
                    g, t = j // T, j % T
                    pe.wait_ge(split, 9 * (e * HALVES + g + 1))
                    if not (first and i == 8):
                        pe.wait_ge(gt_up, m)
                    for s in range(3):
                        at_ = (t % 4 * 2 + t // 4) * TEAR
                        ins = nc.tensor.transpose(PS[0:TEAR, 7, s * P // 2:(s + 1) * P // 2].bitcast(BF16),
                                                  G34P[:, g, s, at_:at_ + TEAR], IDB)
                    ins.then_inc(gt_mm, 1)
                if lagged(i, 9, first, last):
                    j, m = (i - 9) % STEPS, at(b, i - 9)
                    e = b if i >= 9 else b - 1
                    g = j // T
                    pe.wait_ge(gt_up, m + 1)
                    pe.wait_ge(row_in[j % ROWS], (e * (STEPS // ROWS) + j // ROWS + 1) * 16)
                    for gr in range(G2):
                        if not (first and i == 9 and gr < 2):
                            pe.wait_ge(a_up, m * G2 + gr - 1)
                        for ch in range(3 * gr, min(CHUNKS, 3 * gr + 3)):
                            dst = PS[:, (3 * j + gr) % 2 * 3 + ch - 3 * gr, 0:CH]
                            cols = slice(ch * CH, (ch + 1) * CH)
                            for s in range(3):
                                k = TEAR + 3 if s == 0 else TEAR
                                nc.tensor.matmul(dst, GT[0:k, j % 2, s, :], SELR[0:k, j % ROWS, cols], start=(s == 0),
                                                 stop=False)
                            for s in range(3):
                                ins = nc.tensor.matmul(dst, IDB, G2P[:, g, s, cols], start=False, stop=(s == 2))
                        ins.then_inc(gates_mm, 1)

            run(pe, step2)


def constants(B):
    f = np.float32
    eye = np.eye(P)
    blockdiag = np.kron(np.eye(P // GROUP), np.ones((GROUP, GROUP))) / GROUP
    sq = np.stack([eye, -blockdiag / HW, (blockdiag - eye) / HW, blockdiag], 1)
    mask = np.zeros((CIN, 4, 3, CT))
    for d in range(3):
        for c in range(CT):
            mask[c + d, :, d, c] = 1
    mask1 = np.zeros((2, H, 3, H))
    for d in range(3):
        for h in range(H):
            if 0 <= h + d - 1 < H:
                mask1[:, h + d - 1, d, h] = 1
    kind = np.zeros((P, 8))
    q = np.arange(P)
    first = q % 4 < 2
    kind[:, 0], kind[:, 1], kind[:, 2] = first, ~first / T, ~first / H
    kind[:, 3], kind[:, 4] = q % 2 == 0, q % 2 == 1
    kind[:, 5], kind[:, 6] = q < H, (q >= H) / (P * HALVES)
    gate = np.zeros((P, 24))
    weight = gate[:, 0:16].reshape(P, 4, 2, 2)
    weight[:, 0, 0] = 1 / H
    weight[:, 1:, 0] = CT * (NCT - 1) / (P * HALVES) / MOUT
    weight[:, 1:, 1] = (MLAST // 4) / (P * HALVES) / MLAST
    gate[:, 0:16] = weight.reshape(P, 16)
    valid = np.zeros((P, 4, 2))
    valid[:, 0, 0] = q < H
    valid[:, 1:, 0] = (q < MOUT)[:, None]
    valid[:, 1:, 1] = (q < MLAST)[:, None]
    gate[:, 16:] = valid.reshape(P, 8)
    sel = np.zeros((2, W, H, W))
    for a in range(W):
        sel[0, a, :, a] = 1
        sel[1, a, a, :] = 1
    return [("k_sq", sq.astype(f)), ("k_mask", mask.reshape(KIN, 3, CT).astype(f)),
            ("k_mask1", mask1.reshape(2 * H, 3, H).astype(f)), ("k_kind", kind.astype(f)), ("k_gate", gate.astype(f)),
            ("k_sel", sel.reshape(TEAR, HW).astype(f))]


def kernel(x, L0_conv_w_str, L0_conv_w_sr, L0_conv_w_trh, L0_conv_w_trw, L0_conv_gamma, L0_conv_beta):
    from concourse import bacc
    from concourse.bass_utils import run_bass_kernel_spmd

    arrays = [("x", x), ("w_str", L0_conv_w_str), ("w_sr", L0_conv_w_sr), ("w_trh", L0_conv_w_trh),
              ("w_trw", L0_conv_w_trw), ("gamma", L0_conv_gamma), ("beta", L0_conv_beta)]
    arrays += constants(x.shape[0] // T)
    nc = bacc.Bacc("TRN2", target_bir_lowering=False, num_devices=1)
    feed, args = {}, []
    for name, a in arrays:
        a = np.ascontiguousarray(a)
        feed[name] = a
        args.append(nc.dram_tensor(name, a.shape, mybir.dt.from_np(a.dtype), kind="ExternalInput").ap())
    out = nc.dram_tensor("out", x.shape, F32, kind="ExternalOutput").ap()
    build(nc, *args, out)
    r = run_bass_kernel_spmd(nc, [feed], core_ids=[0])
    return r.results[0]["out"]
```
